# Optimizing a Trainium2 kernel written in Bass

```python
import numpy as np
import jax
import jax.numpy as jnp

def _softmax(x, axis=-1):
    return jax.nn.softmax(x, axis=axis)

def _gelu(x):
    return jax.nn.gelu(x, approximate=True)

def _silu(x):
    return jax.nn.silu(x)

def _sigmoid(x):
    return jax.nn.sigmoid(x)

def _layernorm(x, axis=-1, eps=1e-05):
    m = jnp.mean(x, axis=axis, keepdims=True)
    v = jnp.var(x, axis=axis, keepdims=True)
    return (x - m) / jnp.sqrt(v + eps)

def _scatter_add(tgt, idx, src, axis=0):
    return tgt.at[idx].add(src)

def _segment_sum(src, seg, n):
    return jax.ops.segment_sum(src, seg, n)
kernel_name = 'mk_seq_postln_d1_jaxref_r8_ef3ef9'

def setup_inputs(seed: int=0):
    np.random.seed(seed)
    _w = jnp.asarray

    def _L0_attn_setup():
        import jax, jax.numpy as jnp
        import numpy as np
        HIDDEN = 512
        NHQ = 32
        NHKV = 8
        HEAD_DIM = HIDDEN // NHQ
        THETA = 10000.0

        def _rope(x, theta_base):
            b, h, s, d = x.shape
            inv_freq = 1.0 / theta_base ** (jnp.arange(0, d, 2, dtype=jnp.float32)[:d // 2] / d)
            freqs = jnp.arange(s, dtype=jnp.float32)[:, None] * inv_freq[None, :]
            cos = jnp.cos(freqs).astype(x.dtype)
            sin = jnp.sin(freqs).astype(x.dtype)
            x1, x2 = (x[..., :d // 2], x[..., d // 2:])
            return jnp.concatenate([x1 * cos - x2 * sin, x2 * cos + x1 * sin], axis=-1)
        key = jax.random.key(seed)
        ks = jax.random.split(key, 5)
        std = 1.0 / np.sqrt(HIDDEN)
        x = jax.random.normal(ks[0], (2, 256, HIDDEN), dtype=jnp.float32)
        Wq = jax.random.normal(ks[1], (HIDDEN, HIDDEN), dtype=jnp.float32) * std
        Wk = jax.random.normal(ks[2], (HIDDEN, NHKV * HEAD_DIM), dtype=jnp.float32) * std
        Wv = jax.random.normal(ks[3], (HIDDEN, NHKV * HEAD_DIM), dtype=jnp.float32) * std
        Wo = jax.random.normal(ks[4], (HIDDEN, HIDDEN), dtype=jnp.float32) * std
        return {'x': x, 'Wq': Wq, 'Wk': Wk, 'Wv': Wv, 'Wo': Wo}
    _L0_attn_in = _L0_attn_setup()

    def _L0_ffn_setup():
        import jax, jax.numpy as jnp
        import numpy as np
        TOP_K = 2
        key = jax.random.key(seed)
        k0, k1, k2 = jax.random.split(key, 3)
        B, S, D, H, E = (4, 256, 512, 512, 8)
        sc = 1.0 / np.sqrt(D).astype(np.float32)
        x = jax.random.normal(k0, (B, S, D), dtype=jnp.float32)
        W_gate = jax.random.normal(k1, (D, E), dtype=jnp.float32) * sc
        b_gate = jnp.zeros((E,), dtype=jnp.float32)
        W_e = jax.random.normal(k2, (E, D, H), dtype=jnp.float32) * sc
        b_e = jnp.zeros((E, H), dtype=jnp.float32)
        return {'x': x, 'W_gate': W_gate, 'b_gate': b_gate, 'W_e': W_e, 'b_e': b_e}
    _L0_ffn_in = _L0_ffn_setup()
    _d = {'L0_attn_x': _L0_attn_in['x'], 'L0_attn_Wq': _L0_attn_in['Wq'], 'L0_attn_Wk': _L0_attn_in['Wk'], 'L0_attn_Wv': _L0_attn_in['Wv'], 'L0_attn_Wo': _L0_attn_in['Wo'], 'L0_ffn_W_gate': _L0_ffn_in['W_gate'], 'L0_ffn_b_gate': _L0_ffn_in['b_gate'], 'L0_ffn_W_e': _L0_ffn_in['W_e'], 'L0_ffn_b_e': _L0_ffn_in['b_e']}
    _x0 = _d['L0_attn_x']
    _d['L0_attn_x'] = jax.random.normal(jax.random.fold_in(jax.random.key(seed), 1), (2, 1024, 512), dtype=_x0.dtype)
    del _x0
    return _d

def reference(L0_attn_x, L0_attn_Wq, L0_attn_Wk, L0_attn_Wv, L0_attn_Wo, L0_ffn_W_gate, L0_ffn_b_gate, L0_ffn_W_e, L0_ffn_b_e):

    def _L0_attn_ref(x, Wq, Wk, Wv, Wo):
        import jax, jax.numpy as jnp
        import numpy as np
        HIDDEN = 512
        NHQ = 32
        NHKV = 8
        HEAD_DIM = HIDDEN // NHQ
        THETA = 10000.0

        def _rope(x, theta_base):
            b, h, s, d = x.shape
            inv_freq = 1.0 / theta_base ** (jnp.arange(0, d, 2, dtype=jnp.float32)[:d // 2] / d)
            freqs = jnp.arange(s, dtype=jnp.float32)[:, None] * inv_freq[None, :]
            cos = jnp.cos(freqs).astype(x.dtype)
            sin = jnp.sin(freqs).astype(x.dtype)
            x1, x2 = (x[..., :d // 2], x[..., d // 2:])
            return jnp.concatenate([x1 * cos - x2 * sin, x2 * cos + x1 * sin], axis=-1)
        b, s, _ = x.shape
        q_per_kv = NHQ // NHKV
        q = (x @ Wq).reshape(b, s, NHQ, HEAD_DIM).transpose(0, 2, 1, 3)
        k = (x @ Wk).reshape(b, s, NHKV, HEAD_DIM).transpose(0, 2, 1, 3)
        v = (x @ Wv).reshape(b, s, NHKV, HEAD_DIM).transpose(0, 2, 1, 3)
        q = _rope(q, THETA)
        k = _rope(k, THETA)
        qg = q.reshape(b, NHKV, q_per_kv, s, HEAD_DIM)
        scores = jnp.einsum('bkgqd,bkmd->bkgqm', qg, k) / np.sqrt(HEAD_DIM)
        causal = jnp.tril(jnp.ones((s, s), dtype=bool))
        scores = jnp.where(causal, scores, -jnp.inf)
        attn = jax.nn.softmax(scores, axis=-1)
        out = jnp.einsum('bkgqm,bkmd->bkgqd', attn, v)
        out = out.reshape(b, NHQ, s, HEAD_DIM).transpose(0, 2, 1, 3).reshape(b, s, HIDDEN)
        return out @ Wo

    def _L0_ffn_ref(x, W_gate, b_gate, W_e, b_e):
        import jax, jax.numpy as jnp
        import numpy as np
        TOP_K = 2
        logits = x @ W_gate + b_gate
        _, top_idx = jax.lax.top_k(logits, TOP_K)
        y_all = jax.nn.relu(jnp.einsum('bsd,edh->bseh', x, W_e) + b_e)
        y = jnp.take_along_axis(y_all, top_idx[..., None], axis=2)
        return y.mean(axis=2)
    x = L0_attn_x
    x = _layernorm(x + _L0_attn_ref(x, L0_attn_Wq, L0_attn_Wk, L0_attn_Wv, L0_attn_Wo), axis=-1)
    x = _layernorm(x + _L0_ffn_ref(x, L0_ffn_W_gate, L0_ffn_b_gate, L0_ffn_W_e, L0_ffn_b_e), axis=-1)
    return x

_drawn_inputs = setup_inputs


def setup_inputs(seed=0):
    import zlib

    import numpy as np

    out = dict(_drawn_inputs(seed))
    spreads = {'L0_ffn_b_gate': (0.0, 0.1), 'L0_ffn_b_e': (0.0, 0.1)}
    factors = {}
    for name, (base, spread) in spreads.items():
        noise = np.random.default_rng([zlib.crc32(name.encode()), seed]).standard_normal(out[name].shape)
        drawn = base * np.exp(spread * noise) if base else spread * noise
        out[name] = jnp.asarray(drawn.astype(out[name].dtype))
    for name, factor in factors.items():
        out[name] = (out[name] * factor).astype(out[name].dtype)
    return out
```

```python
from contextlib import ExitStack

import concourse.bass as bass
from concourse import mybir

F32 = mybir.dt.float32
BF16 = mybir.dt.bfloat16
U32 = mybir.dt.uint32
ALU = mybir.AluOpType
ACT = mybir.ActivationFunctionType
AX = mybir.AxisListType

P = 128
B, S, D = 2, 1024, 512
T = B * S
HQ, HKV, DH = 32, 8, 16
G = HQ // HKV
HALF = DH // 2
E = 8
KC = D // P
QT = S // P
CH = 512
NCHUNK = T // CH
UNITS = B * HKV
SCALE = DH ** -0.5
EPS = 1e-5
MASKED = -3.0e38
QPART = [0, 0, 1, 0, 1, 2]
KPART = [0, 1, 0, 2, 1, 0]
ROWS = len(QPART) * DH
MROW = ROWS
RING = 3
LOADS = 13
STEPS = [(0, kb) for kb in range(4)] + [(1, kb) for kb in range(8)]
NSTEP = len(STEPS)
DIAG = [s for s, (half, kb) in enumerate(STEPS) if kb * P >= half * CH]
VW = 32


def step_cols(s):
    half, kb = STEPS[s]
    return max(kb * P - half * CH, 0)


def q_col(h, q):
    return (q // CH * G + h) * CH + q % CH


def max_uses():
    uses = [[], []]
    for qt in range(QT):
        half, rem = qt // 4, qt % 4
        if half:
            for h in range(G):
                uses[1].append(([(h, qt, 0, CH, 0)], 0))
        n = (rem + 1) * P
        per = {1: 4, 2: 2, 3: 1, 4: 1}[rem + 1]
        for h0 in range(0, G, per):
            uses[half].append(([(h0 + a, qt, half * CH, n, a * n) for a in range(per)], half))
    return uses


MAXUSES = max_uses()


def bank_plan(with_out, with_max):
    seq = []
    if with_max:
        seq = [("mx", 0, u) for u in range(len(MAXUSES[0]))]
        b = [("mx", 1, u) for u in range(len(MAXUSES[1]))]
        seq += b[:3] + [("mt", 0)] + b[3:] + [("mt", 1)]
    if with_out:
        seq.insert(min(2, len(seq)), ("ot", 1, 1))
        seq.insert(min(28, len(seq)), ("ot", 0, 0))
    per = -(-len(seq) * 10 // NSTEP) / 10
    steps = [[] for _ in range(NSTEP)]
    for k, use in enumerate(seq):
        s = min(int(k / per), NSTEP - 1)
        if use == ("ot", 0, 0):
            s = max(s, 8)
        steps[s].append((k, use))
    return seq, steps


SEQ, SEQ_STEPS = bank_plan(True, True)
SEQ_LAST, LAST_STEPS = bank_plan(True, False)
PRO = [u for u in SEQ if u[0] != "ot"]
NUSE, NPRO = len(SEQ), len(PRO)
assert NUSE % 2 == 0 and NPRO % 2 == 0
OT_A = SEQ.index(("ot", 0, 0))
OT_B = SEQ.index(("ot", 1, 1))
MT_AT = [SEQ.index(("mt", 0)), SEQ.index(("mt", 1))]
MT_PRO = [PRO.index(("mt", 0)), PRO.index(("mt", 1))]
LAST_B = SEQ_LAST.index(("ot", 1, 1))
MX_END = [[k for k, u in enumerate(seq) if u[:2] == ("mx", 0)][-1] for seq in (PRO, SEQ)]


def layer(nc, xT, x, wq, wk, wv, wo, wg, bg, we, be, cos, sin, ksin, out):
    ctx = ExitStack()
    with ctx:
        def sb(name, shape, dt):
            return ctx.enter_context(nc.sbuf_tensor(name, shape, dt))

        def sem(name):
            return ctx.enter_context(nc.semaphore(name))

        q_parts = nc.dram_tensor("q_parts", [3, 2, UNITS * HALF, 2, G, CH], BF16, kind="Internal").ap()
        k_parts = nc.dram_tensor("k_parts", [3, 2, UNITS * HALF, S], BF16, kind="Internal").ap()

        attn = sb("attn", [P, (UNITS + 1) * CH + P * 4], F32)
        x_ch = attn[:, 0:2 * KC * CH].rearrange("p (b k t) -> p b k t", b=2, k=KC)
        arena = sb("arena", [P, E * KC * D], F32)
        q_ring = arena[:, 0:6144].bitcast(BF16).rearrange("p (r n) -> p r n", r=RING)
        v_all = arena[:, 6144:10240]
        probs = arena[:, 10240:16384].rearrange("p (b h t) -> p b h t", b=3, h=G)
        we_sb = arena[:, :].rearrange("p (e k n) -> p e k n", e=E, k=KC)
        k_ring = sb("k_ring", [P, RING, S], BF16)
        v_ring = sb("v_ring", [P, RING, QT * VW], F32)
        rope_t = probs[:, 0:2]
        roped = probs[:, 2].rearrange("p (b a) t -> p b a t", b=2)
        resid = sb("resid", [P, 2, 2, CH], F32)
        parts = sb("parts", [P, 2, 3, 2, CH], BF16)
        wq_sb = sb("wq_sb", [P, KC, D], F32)
        wk_sb = sb("wk_sb", [P, KC, P], F32)
        wv_sb = sb("wv_sb", [P, KC, P], F32)
        cos_sb = sb("cos_sb", [P, S], F32)
        sin_sb = sb("sin_sb", [P, S], F32)
        ksin_sb = sb("ksin_sb", [P, S], F32)
        ident = sb("ident", [P, P], F32)
        identb = sb("identb", [P, P], BF16)
        mask = sb("mask", [P, G, P], BF16)
        o_sb = sb("o_sb", [P, 2, CH], F32)
        rden = sb("rden", [P, 2, 16], F32)
        pmax = sb("pmax", [P, 16, 2], F32)
        nmax = sb("nmax", [P, 2, 16], F32)
        nres = sb("nres", [P, 2, 2, 16], F32)
        nparts = sb("nparts", [P, 2, 48], BF16)
        mt_sb = sb("mt_sb", [48, 2, P], BF16)
        wo_sb = sb("wo_sb", [P, KC, D], F32)
        wg_sb = sb("wg_sb", [P, KC, E], F32)
        be_sb = sb("be_sb", [1, E, D], F32)
        bg_sb = sb("bg_sb", [P, E], F32)
        eidx = sb("eidx", [P, E], F32)
        ones = sb("ones", [1, P], F32)
        eps_sb = sb("eps_sb", [P, 1], F32)
        a_tok = sb("a_tok", [P, D], F32)
        a_T = sb("a_T", [P, KC, P], F32)
        x_T = sb("x_T", [P, KC, P], F32)
        x_res = sb("x_res", [P, D], F32)
        z = sb("z", [P, D], F32)
        x1 = sb("x1", [P, D], F32)
        act_e = sb("act_e", [P, 2, D], F32)
        acc = sb("acc", [P, D], F32)
        y_out = sb("y_out", [P, D], F32)
        stat = sb("stat", [P, 2, 6], F32)
        mv = sb("mv", [P, 2, 2], F32)
        rstd = sb("rstd", [P, 2, 2], F32)
        logit = sb("logit", [P, E], F32)
        top = sb("top", [P, 8], F32)
        topi = sb("topi", [P, 8], U32)
        topf = sb("topf", [P, 8], F32)
        gate = sb("gate", [P, 2, E], F32)

        st = ctx.enter_context(nc.psum_tensor("st", [P, G, CH], F32))
        ot = ctx.enter_context(nc.psum_tensor("ot", [P, 2, CH], F32))
        sm = ctx.enter_context(nc.psum_tensor("sm", [P, 2, CH], F32))

        w_loaded = sem("w_loaded")
        x_loaded = [sem(f"x_loaded{p}") for p in range(2)]
        proj_ready = sem("proj_ready")
        v_ready = sem("v_ready")
        v_kept = sem("v_kept")
        rope_mul = sem("rope_mul")
        rope_sum = sem("rope_sum")
        part0 = sem("part0")
        res0 = sem("res0")
        part1 = sem("part1")
        part2 = sem("part2")
        stored = [sem(f"stored{p}") for p in range(2)]
        const_ready = sem("const_ready")
        const_step = sem("const_step")
        loaded = [sem(f"loaded{r}") for r in range(RING)]
        sm_ready = sem("sm_ready")
        sm_free = sem("sm_free")
        nmax_ready = sem("nmax_ready")
        nsplit = sem("nsplit")
        nparts_ready = sem("nparts_ready")
        mrow_set = [sem(f"mrow_set{h}") for h in range(2)]
        st_ready = sem("st_ready")
        exp_done = sem("exp_done")
        masked = sem("masked")
        pv_done = sem("pv_done")
        o_kept = sem("o_kept")
        alone = sem("alone")
        dve_own = sem("dve_own")
        attn_done = sem("attn_done")
        w3_loaded = sem("w3_loaded")
        we_loaded = sem("we_loaded")
        a_ready = sem("a_ready")
        tr_ready = sem("tr_ready")
        tr_kept = sem("tr_kept")
        xr_loaded = sem("xr_loaded")
        y_ready = sem("y_ready")
        own3 = sem("own3")
        var_ready = sem("var_ready")
        std_ready = sem("std_ready")
        x1_ready = sem("x1_ready")
        logit_ready = sem("logit_ready")
        gate_ready = sem("gate_ready")
        e_ready = sem("e_ready")
        relu_done = sem("relu_done")
        acc_done = sem("acc_done")
        y_done = sem("y_done")
        y_stored = sem("y_stored")

        block = ctx.enter_context(nc.Block())
        NPART = 6 * 16

        def rope_units():
            return [(3 * p + u, p, u) for p in range(2) for u in range(3)]

        @block.sync
        def _(sp):
            for t, src in ((wq_sb, wq), (wk_sb, wk), (wv_sb, wv)):
                sp.dma_start(t[:, :, :], src.rearrange("(k p) n -> p k n", p=P)).then_inc(w_loaded, 16)
            for t, src in ((cos_sb, cos), (sin_sb, sin), (ksin_sb, ksin)):
                sp.dma_start(t[:, :], src).then_inc(w_loaded, 16)
            for c in range(NCHUNK):
                if c >= 2:
                    sp.wait_ge(v_ready, c - 1)
                sp.dma_start(x_ch[:, c % 2], xT[:, c * CH:(c + 1) * CH].rearrange("(k p) t -> p k t", p=P)
                             ).then_inc(x_loaded[c % 2], 16)
            sp.dma_start(wo_sb[:, :, :], wo.rearrange("(k p) n -> p k n", p=P)).then_inc(w3_loaded, 16)
            sp.dma_start(wg_sb[:, :, :], wg.rearrange("(k p) n -> p k n", p=P)).then_inc(w3_loaded, 16)
            sp.dma_start(be_sb[:, :, :], be.rearrange("(a e) n -> a e n", a=1)).then_inc(w3_loaded, 16)
            sp.dma_start(bg_sb[:, :], bg.rearrange("(a e) -> a e", a=1).to_broadcast([P, E])).then_inc(w3_loaded, 16)

            def load_unit(n, r):
                for g in range(len(QPART)):
                    rows = slice(g * DH, (g + 1) * DH)
                    src = q_parts[QPART[g], :, bass.ds(n * HALF, HALF)].rearrange("a d x h s -> a d (x h s)")
                    sp.dma_start(q_ring[rows, r], src).then_inc(loaded[r], 16)
                    sp.dma_start(k_ring[rows, r], k_parts[KPART[g], :, bass.ds(n * HALF, HALF)]).then_inc(loaded[r], 16)
                sp.dma_start(v_ring[:, r], v_all[:, bass.ds(n * QT * VW, QT * VW)]).then_inc(loaded[r], 16)

            def max_rows(n, r, mt_at, base):
                for half in range(2):
                    sp.wait_ge(sm_free, base + mt_at[half] + 1)
                    dst = q_ring[MROW:MROW + 3, r, half * G * CH:(half + 1) * G * CH].rearrange("k (c t) -> k c t", t=P)
                    sp.dma_start(dst, mt_sb[:, half, :]).then_inc(mrow_set[half], 16)

            for p in range(2):
                sp.wait_ge(stored[p], 16 + NPART * 6)
            sp.wait_ge(v_kept, NCHUNK + 2)
            for n in range(RING):
                load_unit(n, n)
            max_rows(0, 0, MT_PRO, 0)

            def unit(n, r, load):
                max_rows(n + 1, (r + 1) % RING, MT_AT, NPRO + n * NUSE)
                if load:
                    sp.wait_ge(pv_done, n * NSTEP + NSTEP + 3)
                    load_unit(n + RING, r)

            with sp.Fori(0, 4) as i:
                for k in range(RING):
                    unit(i * RING + k, k, True)
            unit(12, 0, True)
            unit(13, 1, False)
            unit(14, 2, False)

            sp.wait_ge(attn_done, 1)
            sp.dma_start(we_sb[:, :, :, :], we.rearrange("e (k p) n -> p e k n", p=P)).then_inc(we_loaded, 16)
            with sp.Fori(0, T // P) as t:
                sp.wait_ge(y_done, t + 1)
                sp.dma_start(x_res[:, :], x[bass.ds(t * P, P), :]).then_inc(xr_loaded, 16)
                sp.wait_ge(y_done, t + 2)
                sp.dma_start(out[bass.ds(t * P, P), :], y_out[:, :]).then_inc(y_stored, 16)
            sp.wait_ge(y_stored, 16 * (T // P) + 16)

        @block.gpsimd
        def _(pool):
            pool.memset(ident[:, :], 0.0).then_inc(const_step, 1)
            pool.memset(identb[:, :], 0.0).then_inc(const_step, 1)
            pool.memset(mask[:, :, :], 0.0).then_inc(const_step, 1)
            pool.wait_ge(const_step, 3)
            for m in (ident, identb):
                pool.affine_select(out=m[:, :], in_=m[:, :], compare_op=ALU.not_equal, fill=1.0, base=0,
                                   pattern=[[-1, P]], channel_multiplier=1).then_inc(const_ready, 1)
            pool.affine_select(out=mask[:, :, :], in_=mask[:, :, :], compare_op=ALU.is_ge, fill=MASKED,
                               base=0, pattern=[[0, G], [-1, P]], channel_multiplier=1).then_inc(const_ready, 1)
            pool.memset(v_all[:, :], 1.0).then_inc(const_ready, 1)
            pool.iota(eidx[:, :], pattern=[[1, E]], base=0, channel_multiplier=0,
                      allow_small_or_imprecise_dtypes=True).then_inc(const_ready, 1)

            with pool.Fori(0, B) as b:
                for u6, p, u in rope_units():
                    U = b * 6 + u6
                    par = u6 % 2
                    pool.wait_ge(rope_mul, U + 1 + 3)
                    pool.wait_ge(part0, U + 1)
                    pool.wait_ge(res0, U + 1)
                    a = rope_t[:, par]
                    if u < 2:
                        pool.tensor_tensor(roped[:, par, 0], a[:, 0], a[:, 1], ALU.subtract)
                        pool.tensor_tensor(roped[:, par, 1], a[:, 2], a[:, 3], ALU.add).then_inc(rope_sum, 1)
                    else:
                        pool.tensor_tensor(roped[:, par, 0], a[:, 0], a[:, 1], ALU.add).then_inc(rope_sum, 1)

            def settle():
                pool.sem_inc(alone, 1)

            def split_max(half, m, seen):
                pool.wait_ge(*seen)
                settle()
                nm = nmax[:, half]
                c = m * 4
                pool.tensor_copy(nparts[:, half, 0:16], nm).then_inc(nsplit, 1)
                pool.wait_ge(nsplit, c + 1)
                pool.tensor_tensor(nres[:, half, 0], nm, nparts[:, half, 0:16], ALU.subtract).then_inc(nsplit, 1)
                pool.wait_ge(nsplit, c + 2)
                settle()
                pool.tensor_copy(nparts[:, half, 16:32], nres[:, half, 0]).then_inc(nsplit, 1)
                pool.wait_ge(nsplit, c + 3)
                pool.tensor_tensor(nres[:, half, 1], nres[:, half, 0], nparts[:, half, 16:32], ALU.subtract
                                   ).then_inc(nsplit, 1)
                pool.wait_ge(nsplit, c + 4)
                settle()
                pool.tensor_copy(nparts[:, half, 32:48], nres[:, half, 1]).then_inc(nparts_ready, 1)

            split_max(0, 0, (sm_free, MX_END[0] + 1))
            split_max(1, 1, (nmax_ready, 1))

            def unit(n, with_max):
                split_after = {}
                if with_max:
                    for half in range(2):
                        at = [s for s in range(NSTEP) for _, use in SEQ_STEPS[s] if use[:2] == ("mx", half)][-1]
                        split_after[min(at, NSTEP - 1)] = half
                for s in range(NSTEP):
                    if s in DIAG:
                        pool.wait_ge(exp_done, n * (2 * NSTEP) + 2 * s + 2 + 2)
                        settle()
                        d = probs[:, s % 3, :, 0:P]
                        pool.affine_select(out=d, in_=d, compare_op=ALU.is_ge, fill=0.0, base=0,
                                           pattern=[[0, G], [1, P]], channel_multiplier=-1).then_inc(masked, 1)
                    if s in split_after:
                        half = split_after[s]
                        split_max(half, n * 2 + 2 + half,
                                  (nmax_ready, n + 2) if half else (sm_free, NPRO + n * NUSE + MX_END[1] + 1))

            with pool.Fori(0, (UNITS - 1) // RING) as i:
                for k in range(RING):
                    unit(i * RING + k, True)
            unit(UNITS - 1, False)

            pool.wait_ge(attn_done, 1)
            with pool.Fori(0, B) as b:
                with pool.Fori(0, QT) as qt:
                    t = b * QT + qt
                    pool.wait_ge(y_done, t + 1)
                    settle()
                    src = attn[:, bass.ds(CH + b * (HKV * CH) + qt * 64, HKV * CH)].rearrange("p (j c) -> p j c", c=CH)
                    pool.tensor_copy(a_tok[:, :].rearrange("p (j c) -> p j c", c=64), src[:, :, 0:64]
                                     ).then_inc(a_ready, 1)

        @block.scalar
        def _(act):
            act.sem_inc(part0, 2)
            act.sem_inc(part1, 2)
            for p in range(2):
                act.sem_inc(stored[p], 16)
            act.sem_inc(exp_done, 2)
            act.sem_inc(o_kept, 2)

            def store_parts(b, p, u, par):
                s0 = p * CH
                for k in range(3):
                    for a in range(2):
                        if u < 2:
                            dst = q_parts[k, a, bass.ds(b * 64 + u * 32, 32), p].rearrange("r h s -> h r s")
                            src = parts[:, par, k, a, :]
                        else:
                            dst = k_parts[k, a, bass.ds(b * 64, 64), s0:s0 + CH]
                            src = parts[a * 64:(a + 1) * 64, par, k, 0, :]
                        act.dma_start(dst, src).then_inc(stored[par], 16)

            act.sem_inc(v_kept, 2)
            act.wait_ge(const_ready, 9)
            with act.Fori(0, B) as b:
                for u6, p, u in rope_units():
                    U = b * 6 + u6
                    par = u6 % 2
                    w = 2 if u < 2 else 1
                    act.wait_ge(rope_sum, U + 1 + 2)
                    act.wait_ge(stored[par], (b * 3 + u6 // 2) * NPART + 16)
                    nc.scalar.activation(parts[:, par, 0, 0:w], roped[:, par, 0:w], ACT.Copy).then_inc(part0, 1)
                    if u == 2:
                        act.wait_ge(v_ready, b * 2 + p + 1)
                        dst = v_all[:, bass.ds(b * (HKV * QT * VW), HKV * QT * VW)].rearrange(
                            "p (j t c) -> p t j c", j=HKV, t=QT)[:, 4 * p:4 * p + 4, :, 0:DH]
                        for t in range(4):
                            src = sm[:, p, t * P:(t + 1) * P].rearrange("p (j c) -> p j c", c=DH)
                            ins = nc.scalar.activation(dst[:, t], src, ACT.Copy)
                        ins.then_inc(v_kept, 1)
                    act.wait_ge(res0, U + 1 + 2)
                    nc.scalar.activation(parts[:, par, 1, 0:w], resid[:, par, 0:w], ACT.Copy).then_inc(part1, 1)
                    act.wait_ge(part0, U + 1 + 2)
                    act.wait_ge(part1, U + 1 + 2)
                    act.wait_ge(part2, U + 1)
                    store_parts(b, p, u, par)

            def keep_out(half, n):
                nc.scalar.activation(o_sb[:, half], ot[:, half], ACT.Copy).then_inc(o_kept, 1)

            def unit(n, out_at):
                for s in range(NSTEP):
                    c0 = step_cols(s)
                    w = CH - c0
                    for hp in range(2):
                        act.wait_ge(st_ready, n * (2 * NSTEP) + 2 * s + hp + 1)
                        act.wait_ge(pv_done, n * NSTEP + s + 1)
                        nc.scalar.activation(probs[:, s % 3, 2 * hp:2 * hp + 2, 0:w], st[:, 2 * hp:2 * hp + 2, 0:w],
                                             ACT.Exp, scale=SCALE).then_inc(exp_done, 1)
                    if s == 6:
                        act.wait_ge(pv_done, n * NSTEP + 4 + 3)
                        act.wait_ge(sm_ready, NPRO + n * NUSE - NUSE + OT_A + 1)
                        keep_out(0, n)
                act.wait_ge(pv_done, n * NSTEP + NSTEP + 3)
                act.wait_ge(sm_ready, NPRO + n * NUSE + out_at + 1)
                keep_out(1, n)

            with act.Fori(0, (UNITS - 1) // RING) as i:
                for k in range(RING):
                    unit(i * RING + k, OT_B)
            unit(UNITS - 1, LAST_B)

            with act.Fori(0, T // P) as t:
                for which, dst in enumerate((a_T, x_T)):
                    act.wait_ge(tr_ready, t * 2 + which + 1)
                    nc.scalar.activation(dst[:, :, :].rearrange("p k n -> p (k n)"), sm[:, 0], ACT.Copy).then_inc(tr_kept, 1)
                    if which == 0:
                        act.wait_ge(var_ready, t * 2 + 1)
                        nc.scalar.activation(rstd[:, 0, 0:1], mv[:, 0, 1:2], ACT.Sqrt, bias=eps_sb[:, 0:1]
                                             ).then_inc(std_ready, 1)
                act.wait_ge(gate_ready, t + 1)
                for e in range(E):
                    act.wait_ge(e_ready, t * E + e + 1)
                    act.wait_ge(acc_done, t * E + e + 1)
                    nc.scalar.activation(act_e[:, e % 2], st[:, e % 4], ACT.Relu, scale=gate[:, 0, e:e + 1]
                                         ).then_inc(relu_done, 1)
                act.wait_ge(var_ready, t * 2 + 2)
                nc.scalar.activation(rstd[:, 1, 0:1], mv[:, 1, 1:2], ACT.Sqrt, bias=eps_sb[:, 0:1]
                                     ).then_inc(std_ready, 1)

        @block.vector
        def _(dve):
            dve.sem_inc(rope_mul, 3)
            dve.sem_inc(rope_sum, 2)
            dve.sem_inc(res0, 2)
            nc.vector.memset(k_ring[MROW:P, :, :], 1.0).then_inc(const_ready, 1)
            nc.vector.memset(o_sb[:, :, :], 1.0).then_inc(const_ready, 1)
            nc.vector.memset(ones[:, :], 1.0).then_inc(const_ready, 1)
            nc.vector.memset(eps_sb[:, :], EPS).then_inc(const_ready, 1)

            def products(b, u6, p, u):
                U = b * 6 + u6
                par = u6 % 2
                dve.wait_ge(proj_ready, U + 1)
                dve.wait_ge(rope_sum, U + 1)
                t = rope_t[:, par]
                s0 = p * CH
                c, si, ks = (m[:, s0:s0 + CH] for m in (cos_sb, sin_sb, ksin_sb))
                if u < 2:
                    x1_, x2_ = st[:, 2 * u], st[:, 2 * u + 1]
                    nc.vector.tensor_tensor(t[:, 0], x1_, c, ALU.mult)
                    nc.vector.tensor_tensor(t[:, 1], x2_, si, ALU.mult)
                    nc.vector.tensor_tensor(t[:, 2], x2_, c, ALU.mult)
                    nc.vector.tensor_tensor(t[:, 3], x1_, si, ALU.mult).then_inc(rope_mul, 1)
                else:
                    kk = ot[:, p]
                    nc.vector.tensor_tensor(t[:, 0], kk, c, ALU.mult)
                    nc.vector.tensor_tensor(t[0:64, 1], kk[64:128], ks[64:128], ALU.mult)
                    nc.vector.tensor_tensor(t[64:128, 1], kk[0:64], ks[0:64], ALU.mult).then_inc(rope_mul, 1)

            def residual(b, u6, p, u):
                U = b * 6 + u6
                par, w = u6 % 2, 2 if u < 2 else 1
                dve.wait_ge(part0, U + 1 + 2)
                dve.wait_ge(part1, U + 1)
                nc.vector.tensor_tensor(resid[:, par, 0:w], roped[:, par, 0:w], parts[:, par, 0, 0:w], ALU.subtract
                                        ).then_inc(res0, 1)

            def last_part(b, u6, p, u):
                U = b * 6 + u6
                par, w = u6 % 2, 2 if u < 2 else 1
                dve.wait_ge(part1, U + 1 + 2)
                nc.vector.tensor_tensor(parts[:, par, 2, 0:w], resid[:, par, 0:w], parts[:, par, 1, 0:w], ALU.subtract
                                        ).then_inc(part2, 1)

            dve.wait_ge(w_loaded, 96)
            with dve.Fori(0, B) as b:
                us = rope_units()
                for k in range(len(us) + 2):
                    if k < len(us):
                        products(b, *us[k])
                    if 2 <= k:
                        last_part(b, *us[k - 2])
                    if 1 <= k <= len(us):
                        residual(b, *us[k - 1])

            def reduce_use(half, u, idx_par):
                blocks, chunk = MAXUSES[half][u]
                per, (h0, qt, _, n, _) = len(blocks), blocks[0]
                src = sm[:, idx_par, 0:per * n].rearrange("p (h n) -> p h n", n=n)
                rem = qt % 4
                if half == 0:
                    dst = nmax[:, 0, :].rearrange("p (h q) -> p h q", q=4)[:, h0:h0 + per, rem]
                    return nc.vector.tensor_reduce(dst, src, AX.X, ALU.max, negate=True)
                dst = pmax[:, :, chunk].rearrange("p (h q) -> p h q", q=4)[:, h0:h0 + per, rem]
                return nc.vector.tensor_reduce(dst, src, AX.X, ALU.max)

            def use_banks(n, seq, base, sent, own0):
                outs = 0
                for k, use in enumerate(seq):
                    par = k % 2
                    dve.wait_ge(sm_ready, base + k + 1)
                    if use[0] == "mx":
                        reduce_use(use[1], use[2], par).then_inc(sm_free, 1)
                        if use[1] == 1 and use[2] + 1 == len(MAXUSES[1]):
                            dve.wait_ge(sm_free, base + k + 1)
                            nc.vector.tensor_reduce(nmax[:, 1, :], pmax[:, :, :], AX.X, ALU.max, negate=True
                                                    ).then_inc(nmax_ready, 1)
                    elif use[0] == "mt":
                        if sent is not None:
                            dve.wait_ge(mrow_set[use[1]], sent * 16)
                        bank = sm[:, par].bitcast(BF16)
                        nc.vector.tensor_copy(mt_sb[:, use[1], :], bank[0:48, 0:P]).then_inc(sm_free, 1)
                    else:
                        _, half, back = use
                        slot = (n + 1 - back) * CH + half * 256
                        o_t = sm[:, par].rearrange("p (q c) -> p q c", c=VW)
                        nc.vector.reciprocal(rden[:, half, :], o_t[:, :, DH]).then_inc(dve_own, 1)
                        outs += 1
                        dve.wait_ge(dve_own, own0 + outs)
                        nc.vector.tensor_tensor(attn[:, bass.ds(slot, 256)].rearrange("p (q c) -> p q c", c=DH),
                                                o_t[:, :, 0:DH], rden[:, half, :].unsqueeze(2).to_broadcast([P, 16, DH]),
                                                ALU.mult).then_inc(sm_free, 1)

            dve.wait_ge(v_kept, NCHUNK + 2)
            use_banks(0, PRO, 0, None, 0)
            with dve.Fori(0, (UNITS - 1) // RING) as i:
                for k in range(RING):
                    n = i * RING + k
                    use_banks(n, SEQ, NPRO + n * NUSE, n + 1, n * 2)
            use_banks(UNITS - 1, SEQ_LAST + [("ot", 1, 0)], NPRO + (UNITS - 1) * NUSE, None, (UNITS - 1) * 2)
            dve.wait_ge(sm_free, NPRO + (UNITS - 1) * NUSE + len(SEQ_LAST) + 1)
            dve.sem_inc(attn_done, 1)

            dve.sem_inc(y_done, 1)
            dve.sem_inc(y_stored, 16)
            dve.sem_inc(relu_done, 4)
            dve.sem_inc(acc_done, 2)
            dve.wait_ge(w3_loaded, 64)
            OWN = 12

            def normed(t, which, dst, own):
                nc.vector.bn_stats(stat[:, which], z[:, :]).then_inc(own3, 1)
                dve.wait_ge(own3, own + 1)
                dve.sem_inc(alone, 1)
                nc.vector.bn_aggr(mv[:, which], stat[:, which]).then_inc(var_ready, 1)
                dve.wait_ge(std_ready, t * 2 + which + 1)
                nc.vector.reciprocal(rstd[:, which, 1:2], rstd[:, which, 0:1]).then_inc(own3, 1)
                dve.wait_ge(own3, own + 2)
                return nc.vector.tensor_scalar(dst[:, :], z[:, :], mv[:, which, 0:1], rstd[:, which, 1:2],
                                               ALU.subtract, ALU.mult)

            with dve.Fori(0, T // P) as t:
                o = t * OWN
                dve.wait_ge(y_ready, t + 1)
                dve.wait_ge(xr_loaded, t * 16 + 16)
                nc.vector.tensor_tensor(z[:, :], sm[:, 1], x_res[:, :], ALU.add).then_inc(own3, 1)
                dve.wait_ge(own3, o + 1)
                normed(t, 0, x1, o + 1).then_inc(x1_ready, 1)
                dve.wait_ge(logit_ready, t + 1)
                nc.vector.tensor_tensor(logit[:, :], ot[:, 0, 0:E], bg_sb[:, :], ALU.add).then_inc(own3, 1)
                dve.wait_ge(own3, o + 4)
                dve.sem_inc(alone, 1)
                nc.vector.max(top[:, :], logit[:, :]).then_inc(own3, 1)
                dve.wait_ge(own3, o + 5)
                dve.sem_inc(alone, 1)
                nc.vector.max_index(topi[:, :], top[:, :], logit[:, :]).then_inc(own3, 1)
                dve.wait_ge(own3, o + 6)
                nc.vector.tensor_copy(topf[:, :], topi[:, :]).then_inc(own3, 1)
                dve.wait_ge(own3, o + 7)
                nc.vector.tensor_scalar(gate[:, 1, :], eidx[:, :], topf[:, 0:1], 0.5, ALU.is_equal, ALU.mult).then_inc(own3, 1)
                nc.vector.tensor_scalar(logit[:, :], eidx[:, :], topf[:, 1:2], 0.5, ALU.is_equal, ALU.mult).then_inc(own3, 1)
                dve.wait_ge(own3, o + 9)
                nc.vector.tensor_tensor(gate[:, 0, :], gate[:, 1, :], logit[:, :], ALU.add).then_inc(gate_ready, 1)
                for e in range(E):
                    dve.wait_ge(relu_done, t * E + e + 1 + 4)
                    if e == 0:
                        nc.vector.tensor_copy(acc[:, :], act_e[:, 0]).then_inc(acc_done, 1)
                    else:
                        dve.wait_ge(acc_done, t * E + e + 2)
                        nc.vector.tensor_tensor(acc[:, :], acc[:, :], act_e[:, e % 2], ALU.add).then_inc(acc_done, 1)
                dve.wait_ge(acc_done, t * E + E + 2)
                nc.vector.tensor_tensor(z[:, :], x1[:, :], acc[:, :], ALU.add).then_inc(own3, 1)
                dve.wait_ge(own3, o + 10)
                dve.wait_ge(y_stored, t * 16 + 16)
                normed(t, 1, y_out, o + 10).then_inc(y_done, 1)

        @block.tensor
        def _(pe):
            pe.sem_inc(pv_done, 3)
            pe.wait_ge(w_loaded, 96)
            with pe.Fori(0, B) as b:
                for p in range(2):
                    pe.wait_ge(x_loaded[p], b * 16 + 16)
                    for u in range(3):
                        pe.wait_ge(rope_mul, b * 6 + 3 * p + u + 1)
                        outs = [(st[:, 2 * u + a], wq_sb, (2 * u + a) * P) for a in range(2)] if u < 2 else [(ot[:, p], wk_sb, 0)]
                        for dst, w, col in outs:
                            for k in range(KC):
                                ins = nc.tensor.matmul(dst, w[:, k, col:col + P], x_ch[:, p, k], start=k == 0, stop=k == KC - 1)
                        ins.then_inc(proj_ready, 1)
                    pe.wait_ge(v_kept, b * 2 + p + 1)
                    for t in range(4):
                        for k in range(KC):
                            ins = nc.tensor.matmul(sm[:, p, t * P:(t + 1) * P], x_ch[:, p, k, t * P:(t + 1) * P],
                                                   wv_sb[:, k], start=k == 0, stop=k == KC - 1)
                    ins.then_inc(v_ready, 1)

            def bank_use(use, par, n, r, base_k, halves):
                if not isinstance(base_k, int) or base_k >= 2:
                    pe.wait_ge(sm_free, base_k - 1)
                if use[0] == "mx":
                    blocks, chunk = MAXUSES[use[1]][use[2]]
                    per, m = len(blocks), blocks[0][3]
                    diag = chunk == use[1]
                    if diag:
                        out = sm[:, par, 0:per * m].rearrange("p (h n) -> p h n", n=m)[:, :, m - P:m]
                        nc.tensor.matmul(out, identb[:, :], mask[:, 0:per, :], start=True, stop=False, skip_group_check=True)
                    for h, qt, k0, w, col in blocks:
                        ins = nc.tensor.matmul(sm[:, par, col:col + w], q_ring[0:ROWS, r, q_col(h, qt * P):q_col(h, qt * P) + P],
                                               k_ring[0:ROWS, r, k0:k0 + w], start=not diag, stop=True, skip_group_check=True)
                elif use[0] == "mt":
                    pe.wait_ge(nparts_ready, halves + use[1] + 1)
                    pe.sem_inc(alone, 1)
                    ins = nc.tensor.transpose(sm[:, par].bitcast(BF16)[0:48, 0:P], nparts[:, use[1], :], identb[:, :])
                else:
                    _, half, back = use
                    pe.wait_ge(o_kept, 2 + n * 2 + (0 if back else 1 + half))
                    for q in range(4):
                        ins = nc.tensor.transpose(sm[:, par, q * P:(q + 1) * P], o_sb[:, half, q * P:(q + 1) * P], ident[:, :])
                ins.then_inc(sm_ready, 1)

            def scores(n, r, s):
                half, kb = STEPS[s]
                c0 = step_cols(s)
                if s == 0:
                    pe.wait_ge(mrow_set[0], n * 16 + 16)
                if s == 4:
                    pe.wait_ge(mrow_set[1], n * 16 + 16)
                for hp in range(2):
                    pe.wait_ge(exp_done, n * (2 * NSTEP) + 2 * s + hp + 1)
                    for h in (2 * hp, 2 * hp + 1):
                        ins = nc.tensor.matmul(st[:, h, 0:CH - c0], k_ring[0:MROW + 3, r, kb * P:(kb + 1) * P],
                                               q_ring[0:MROW + 3, r, q_col(h, half * CH) + c0:q_col(h, half * CH) + CH],
                                               start=True, stop=True)
                    ins.then_inc(st_ready, 1)

            def weigh(n, r, s):
                half, kb = STEPS[s]
                c0 = step_cols(s)
                if kb == 0:
                    pe.wait_ge(o_kept, n * 2 + 1 + half)
                if s in DIAG:
                    pe.wait_ge(masked, n * len(DIAG) + DIAG.index(s) + 1)
                else:
                    pe.wait_ge(exp_done, n * (2 * NSTEP) + 2 * s + 2 + 2)
                last = kb == (3, 7)[half]
                for h in range(G):
                    ins = nc.tensor.matmul(ot[32 * h:32 * h + 32, half, c0:CH], v_ring[:, r, kb * VW:(kb + 1) * VW],
                                           probs[:, s % 3, h, 0:CH - c0], start=kb == 0, stop=last, skip_group_check=True)
                ins.then_inc(pv_done, 1)

            def unit(n, r, i, seq, steps, next_loads):
                base = NPRO + n * NUSE
                if next_loads is not None:
                    pe.wait_ge(*next_loads)
                for s in range(NSTEP):
                    scores(n, r, s)
                    for k, use in steps[s]:
                        if use != ("mt", 1):
                            bank_use(use, k % 2, n, (r + 1) % RING, base + k, n * 2 + 2)
                    if s:
                        weigh(n, r, s - 1)
                weigh(n, r, NSTEP - 1)
                if ("mt", 1) in seq:
                    bank_use(("mt", 1), MT_AT[1] % 2, n, (r + 1) % RING, base + MT_AT[1], n * 2 + 2)

            pe.wait_ge(const_ready, 9)
            pe.wait_ge(rope_mul, NCHUNK * 3 + 3)
            pe.wait_ge(v_kept, NCHUNK + 2)
            pe.wait_ge(loaded[0], LOADS * 16)
            for k, use in enumerate(PRO):
                bank_use(use, k % 2, 0, 0, k, 0)
            with pe.Fori(0, (UNITS - 1) // RING) as i:
                for k in range(RING):
                    unit(i * RING + k, k, i, SEQ, SEQ_STEPS,
                         (loaded[(k + 1) % RING], (i + (k + 1) // RING) * (LOADS * 16) + LOADS * 16))
            unit(UNITS - 1, 0, None, SEQ_LAST, LAST_STEPS, None)
            k = len(SEQ_LAST)
            bank_use(("ot", 1, 0), k % 2, UNITS - 1, 0, NPRO + (UNITS - 1) * NUSE + k, 0)

            pe.wait_ge(w3_loaded, 64)
            pe.wait_ge(attn_done, 1)
            pe.wait_ge(we_loaded, 16)
            with pe.Fori(0, T // P) as t:
                pe.wait_ge(a_ready, t + 1)
                for k in range(KC):
                    ins = nc.tensor.transpose(sm[:, 0, k * P:(k + 1) * P], a_tok[:, k * P:(k + 1) * P], ident[:, :])
                ins.then_inc(tr_ready, 1)
                pe.wait_ge(tr_kept, t * 2 + 1)
                for k in range(KC):
                    ins = nc.tensor.matmul(sm[:, 1], a_T[:, k], wo_sb[:, k], start=k == 0, stop=k == KC - 1)
                ins.then_inc(y_ready, 1)
                pe.wait_ge(x1_ready, t + 1)
                for k in range(KC):
                    ins = nc.tensor.transpose(sm[:, 0, k * P:(k + 1) * P], x1[:, k * P:(k + 1) * P], ident[:, :])
                ins.then_inc(tr_ready, 1)
                pe.wait_ge(tr_kept, t * 2 + 2)
                for k in range(KC):
                    ins = nc.tensor.matmul(ot[:, 0, 0:E], x_T[:, k], wg_sb[:, k], start=k == 0, stop=k == KC - 1)
                ins.then_inc(logit_ready, 1)
                for e in range(E):
                    pe.wait_ge(relu_done, t * E + e + 1)
                    nc.tensor.matmul(st[:, e % 4], ones[:, :], be_sb[:, e, :], start=True, stop=False)
                    for k in range(KC):
                        ins = nc.tensor.matmul(st[:, e % 4], x_T[:, k], we_sb[:, e, k], start=False, stop=k == KC - 1)
                    ins.then_inc(e_ready, 1)


def kernel(L0_attn_x, L0_attn_Wq, L0_attn_Wk, L0_attn_Wv, L0_attn_Wo, L0_ffn_W_gate, L0_ffn_b_gate, L0_ffn_W_e, L0_ffn_b_e):
    import numpy as np
    import concourse.bacc as bacc
    from concourse.bass_utils import run_bass_kernel_spmd

    x = np.asarray(L0_attn_x).reshape(T, D)
    wq = np.asarray(L0_attn_Wq).reshape(D, 2, 4, G, 2, HALF).transpose(0, 1, 4, 3, 2, 5).reshape(D, D)
    wk = np.asarray(L0_attn_Wk).reshape(D, HKV, 2, HALF).transpose(0, 2, 1, 3).reshape(D, HKV * DH)
    inv = (1.0 / np.float32(10000.0) ** (np.arange(0, DH, 2, dtype=np.float32) / np.float32(DH))).astype(np.float32)
    ang = np.tile((np.arange(S, dtype=np.float32)[:, None] * inv[None, :]).T, (P // HALF, 1))
    cos, sin = np.cos(ang), np.sin(ang)
    ksin = np.where(np.arange(P)[:, None] < 64, sin, -sin)
    data = {
        "xT": x.T, "x": x, "wq": wq, "wk": wk, "wv": L0_attn_Wv, "wo": L0_attn_Wo, "wg": L0_ffn_W_gate,
        "bg": L0_ffn_b_gate, "we": L0_ffn_W_e, "be": L0_ffn_b_e, "cos": cos, "sin": sin, "ksin": ksin,
    }
    nc = bacc.Bacc("TRN2", target_bir_lowering=False, num_devices=1)
    arrays, args = {}, []
    for name, a in data.items():
        a = np.ascontiguousarray(a)
        arrays[name] = a
        args.append(nc.dram_tensor(name, a.shape, mybir.dt.from_np(a.dtype), kind="ExternalInput").ap())
    out = nc.dram_tensor("out", [T, D], F32, kind="ExternalOutput").ap()
    layer(nc, *args, out)
    r = run_bass_kernel_spmd(nc, [arrays], core_ids=[0])
    return np.asarray(r.results[0]["out"]).reshape(B, S, D)
```

```python
from contextlib import ExitStack

import concourse.bass as bass
from concourse import mybir

F32 = mybir.dt.float32
BF16 = mybir.dt.bfloat16
U32 = mybir.dt.uint32
I32 = mybir.dt.int32
ALU = mybir.AluOpType
ACT = mybir.ActivationFunctionType
AX = mybir.AxisListType

P = 128
B, S, D = 2, 1024, 512
T = B * S
HQ, HKV, DH = 32, 8, 16
G = HQ // HKV
HALF = DH // 2
E = 8
KC = D // P
QT = S // P
CH = 512
NCHUNK = T // CH
UNITS = B * HKV
SCALE = DH ** -0.5
EPS = 1e-5
MASKED = -3.0e38
QPART = [0, 0, 1, 0, 1, 2]
KPART = [0, 1, 0, 2, 1, 0]
ROWS = len(QPART) * DH
MROW = ROWS
RING = 3
LOADS = 13
STEPS = [(0, kb) for kb in range(4)] + [(1, kb) for kb in range(8)]
NSTEP = len(STEPS)
DIAG = [s for s, (half, kb) in enumerate(STEPS) if kb * P >= half * CH]
TILES = 2 * T // P + E - 1
NT = T // P
REG = T + P
VW = 32


def step_cols(s):
    half, kb = STEPS[s]
    return max(kb * P - half * CH, 0)


def q_col(h, q):
    return (q // CH * G + h) * CH + q % CH


def max_uses():
    uses = [[], []]
    for qt in range(QT):
        half, rem = qt // 4, qt % 4
        if half:
            for h in range(G):
                uses[1].append(([(h, qt, 0, CH, 0)], 0))
        n = (rem + 1) * P
        per = {1: 4, 2: 2, 3: 1, 4: 1}[rem + 1]
        for h0 in range(0, G, per):
            uses[half].append(([(h0 + a, qt, half * CH, n, a * n) for a in range(per)], half))
    return uses


MAXUSES = max_uses()


def bank_uses(with_max, last_out):
    seq = [("mx", 0, u) for u in range(len(MAXUSES[0]))] if with_max else []
    b = [("mx", 1, u) for u in range(len(MAXUSES[1]))] if with_max else []
    if with_max:
        seq += b[:3] + [("mt", 0)] + b[3:]
    if last_out:
        seq.insert(min(3, len(seq)), ("ot", 1, 1))
        seq.append(("ot", 0, 0))
    if with_max:
        seq.append(("mt", 1))
    return seq


def use_costs(use):
    if use[0] == "mx":
        cols = sum(b[3] for b in MAXUSES[use[1]][use[2]][0])
        return cols, 2.5 * (cols + 60)
    return (128, 400) if use[0] == "mt" else (512, 1700)


def body_plan(seq, ahead):
    pieces = []
    for s in range(2, NSTEP + 2):
        w = CH - step_cols(s % NSTEP)
        if s < NSTEP or ahead:
            pieces += [(("scores", s, 0), 2 * w), (("scores", s, 1), 2 * w)]
        pieces.append((("weigh", s - 2), 4.3 * (CH - step_cols(s - 2))))
    pe_total = sum(c for _, c in pieces) + sum(use_costs(u)[0] for u in seq)
    dve_total = sum(use_costs(u)[1] for u in seq)
    order, pe, dve, k = [], 0, 0, 0
    for piece, cost in pieces:
        order.append(piece)
        pe += cost
        while k < len(seq) and dve * pe_total <= pe * dve_total:
            if seq[k] == ("ot", 0, 0) and ("weigh", 5) not in order:
                break
            order.append(("use", k))
            pe += use_costs(seq[k])[0]
            dve += use_costs(seq[k])[1]
            k += 1
    return order + [("use", j) for j in range(k, len(seq))]


SEQ = bank_uses(True, True)
SEQ_LAST = bank_uses(False, True)
PLAN, PLAN_LAST = body_plan(SEQ, True), body_plan(SEQ_LAST, False)
PRO = bank_uses(True, False)
NUSE, NPRO = len(SEQ), len(PRO)
assert NUSE % 2 == 0 and NPRO % 2 == 0
OT_A = SEQ.index(("ot", 0, 0))
OT_B = SEQ.index(("ot", 1, 1))
MT_AT = [SEQ.index(("mt", 0)), SEQ.index(("mt", 1))]
MT_PRO = [PRO.index(("mt", 0)), PRO.index(("mt", 1))]
LAST_B = SEQ_LAST.index(("ot", 1, 1))
MX1_END = SEQ.index(("mx", 1, len(MAXUSES[1]) - 1))
MX_END = [[k for k, u in enumerate(seq) if u[:2] == ("mx", 0)][-1] for seq in (PRO, SEQ)]


def layer(nc, xT, x, wq, wk, wv, wo, wg, bg, we, be, cos, sin, ksin, out):
    ctx = ExitStack()
    with ctx:
        def sb(name, shape, dt):
            return ctx.enter_context(nc.sbuf_tensor(name, shape, dt))

        def sem(name):
            return ctx.enter_context(nc.semaphore(name))

        q_parts = nc.dram_tensor("q_parts", [3, 2, UNITS * HALF, 2, G, CH], BF16, kind="Internal").ap()
        k_parts = nc.dram_tensor("k_parts", [3, 2, UNITS * HALF, S], BF16, kind="Internal").ap()
        routed = nc.dram_tensor("routed", [E * REG, D], F32, kind="Internal").ap()
        experts_out = nc.dram_tensor("experts_out", [TILES * P, D], F32, kind="Internal").ap()

        attn = sb("attn", [P, (UNITS + 1) * CH + P * 4], F32)
        x_ch = attn[:, 0:2 * KC * CH].rearrange("p (b k t) -> p b k t", b=2, k=KC)
        arena = sb("arena", [P, E * KC * D], F32)
        q_ring = arena[:, 0:6144].bitcast(BF16).rearrange("p (r n) -> p r n", r=RING)
        v_all = arena[:, 6144:10240]
        probs = arena[:, 10240:16384].rearrange("p (b h t) -> p b h t", b=3, h=G)
        we_sb = arena[:, :].rearrange("p (e k n) -> p e k n", e=E, k=KC)
        early = sb("early", [P, 12288], F32)
        wq_sb = early[:, 0:2048].rearrange("p (k n) -> p k n", k=KC)
        wk_sb = early[:, 2048:2560].rearrange("p (k n) -> p k n", k=KC)
        wv_sb = early[:, 2560:3072].rearrange("p (k n) -> p k n", k=KC)
        cos_sb, sin_sb, ksin_sb = (early[:, 3072 + S * i:3072 + S * (i + 1)] for i in range(3))
        resid = early[:, 6144:8192].rearrange("p (b a t) -> p b a t", b=2, a=2)
        parts = early[:, 8192:11264].bitcast(BF16).rearrange("p (b k a t) -> p b k a t", b=2, k=3, a=2)
        x1_all = early[:, 0:NT * D]
        xs = early[:, 8192:9216].rearrange("p (b n) -> p b n", b=2)
        xs_T = early[:, 9216:10240].rearrange("p (b k n) -> p b k n", b=2, k=KC)
        y_b = early[:, 10240:11264].rearrange("p (b n) -> p b n", b=2)
        y_r = early[:, 11264:12288].rearrange("p (b n) -> p b n", b=2)
        be_sb = attn[:, 0:E * D]
        got = attn[:, 4096:6144].rearrange("p (b k n) -> p b k n", b=2, k=2)
        y_out = attn[:, 6144:7168].rearrange("p (b n) -> p b n", b=2)
        k_ring = sb("k_ring", [P, RING, S], BF16)
        v_ring = sb("v_ring", [P, RING, QT * VW], F32)
        rope_t = probs[:, 0:2]
        roped = probs[:, 2].rearrange("p (b a) t -> p b a t", b=2)
        ident = sb("ident", [P, P], F32)
        identb = sb("identb", [P, P], BF16)
        mask = sb("mask", [P, G, P], BF16)
        o_sb = sb("o_sb", [P, 2, CH], F32)
        rden = sb("rden", [P, 2, 16], F32)
        pmax = sb("pmax", [P, 16, 2], F32)
        nmax = sb("nmax", [P, 2, 16], F32)
        nres = sb("nres", [P, 2, 2, 16], F32)
        nparts = sb("nparts", [P, 2, 48], BF16)
        mt_sb = sb("mt_sb", [48, 2, P], BF16)
        wo_sb = sb("wo_sb", [P, KC, D], F32)
        wg_sb = sb("wg_sb", [P, KC, E], F32)
        bg_sb = sb("bg_sb", [P, E], F32)
        eidx = sb("eidx", [P, 2, E], F32)
        eoff = sb("eoff", [P, E], F32)
        before = sb("before", [P, P], BF16)
        ones = sb("ones", [P, P], BF16)
        zeros = sb("zeros", [P, D], F32)
        eps_sb = sb("eps_sb", [P, 1], F32)
        a_tok = sb("a_tok", [P, 2, D], F32)
        a_T = sb("a_T", [P, KC, P], F32)
        x_T = sb("x_T", [P, KC, P], F32)
        x_res = sb("x_res", [P, 2, D], F32)
        z = sb("z", [P, D], F32)
        x1 = sb("x1", [P, 2, D], F32)
        x1_out = sb("x1_out", [P, 2, D], F32)
        stat = sb("stat", [P, 6], F32)
        mv = sb("mv", [P, 2], F32)
        rstd = sb("rstd", [P, 2], F32)
        logit = sb("logit", [P, E], F32)
        top = sb("top", [P, 8], F32)
        topi = sb("topi", [P, 8], U32)
        topf = sb("topf", [P, 8], F32)
        hot = sb("hot", [P, 2, E], F32)
        chosen = sb("chosen", [P, 2, E], BF16)
        sofar = sb("sofar", [P, 2, E], BF16)
        rank = sb("rank", [P, E], F32)
        hrank = sb("hrank", [P, 2, E], F32)
        posf = sb("posf", [P, 2], F32)
        pos = sb("pos", [P, 2, 2], U32)
        pos_all = sb("pos_all", [P, NT, 2], U32)
        gpos = sb("gpos", [P, 2, 2], U32)
        steps128 = sb("steps128", [P, E, NT], F32)
        upto = sb("upto", [P, E, E], F32)
        tnum = sb("tnum", [1, TILES, E], F32)
        many = sb("many", [P, E, NT], F32)
        ntile = sb("ntile", [P, E], F32)
        cumw = sb("cumw", [P, E, E], F32)
        cend = sb("cend", [P, E], F32)
        shift = sb("shift", [P, E], F32)
        hot_all = sb("hot_all", [P, NT * 2, E], F32)
        posf_all = sb("posf_all", [P, NT * 2], F32)
        past = sb("past", [1, TILES, E], F32)
        pastn = sb("pastn", [1, TILES, E], F32)
        te = sb("te", [1, 4, TILES], F32)
        tab = sb("tab", [1, 2, TILES], I32)
        padtab = sb("padtab", [1, E], I32)

        st = ctx.enter_context(nc.psum_tensor("st", [P, G, CH], F32))
        ot = ctx.enter_context(nc.psum_tensor("ot", [P, 2, CH], F32))
        sm = ctx.enter_context(nc.psum_tensor("sm", [P, 2, CH], F32))

        w_loaded = sem("w_loaded")
        x_loaded = [sem(f"x_loaded{p}") for p in range(2)]
        proj_ready = sem("proj_ready")
        v_ready = sem("v_ready")
        v_kept = sem("v_kept")
        rope_mul = sem("rope_mul")
        rope_sum = sem("rope_sum")
        part0 = sem("part0")
        res0 = sem("res0")
        part1 = sem("part1")
        part2 = sem("part2")
        stored = [sem(f"stored{p}") for p in range(2)]
        const_ready = sem("const_ready")
        const_step = sem("const_step")
        loaded = [sem(f"loaded{r}") for r in range(RING)]
        sm_ready = sem("sm_ready")
        sm_free = sem("sm_free")
        nmax_ready = sem("nmax_ready")
        nsplit = sem("nsplit")
        nparts_ready = sem("nparts_ready")
        mrow_set = [sem(f"mrow_set{h}") for h in range(2)]
        st_ready = sem("st_ready")
        exp_done = sem("exp_done")
        masked = sem("masked")
        pv_done = sem("pv_done")
        o_kept = sem("o_kept")
        alone = sem("alone")
        dve_own = sem("dve_own")
        attn_done = sem("attn_done")
        w3_loaded = sem("w3_loaded")
        we_loaded = sem("we_loaded")
        a_ready = sem("a_ready")
        trA_ready = sem("trA_ready")
        trA_kept = sem("trA_kept")
        trX_ready = sem("trX_ready")
        trX_kept = sem("trX_kept")
        xr_loaded = [sem(f"xr_loaded{p}") for p in range(2)]
        y_ready = sem("y_ready")
        z_done = sem("z_done")
        own3 = sem("own3")
        var_ready = sem("var_ready")
        std_ready = sem("std_ready")
        x1_ready = sem("x1_ready")
        x1_kept = sem("x1_kept")
        logit_ready = sem("logit_ready")
        chosen_ready = sem("chosen_ready")
        rank_ready = sem("rank_ready")
        pos_ready = sem("pos_ready")
        sent = [sem(f"sent{p}") for p in range(2)]
        x1_copied = sem("x1_copied")
        count_ready = sem("count_ready")
        tab_ready = sem("tab_ready")
        padded = sem("padded")
        xs_loaded = [sem(f"xs_loaded{p}") for p in range(2)]
        xsT_ready = sem("xsT_ready")
        xsT_kept = sem("xsT_kept")
        e_ready = sem("e_ready")
        yb_done = sem("yb_done")
        yr_done = sem("yr_done")
        y_sent = [sem(f"y_sent{p}") for p in range(2)]
        gpos_ready = sem("gpos_ready")
        got_rows = [sem(f"got_rows{p}") for p in range(2)]
        summed = sem("summed")
        y_done = sem("y_done")
        y_stored = [sem(f"y_stored{p}") for p in range(2)]

        block = ctx.enter_context(nc.Block())
        NPART = 6 * 16

        def rope_units():
            return [(3 * p + u, p, u) for p in range(2) for u in range(3)]

        @block.sync
        def _(sp):
            for t, src in ((wq_sb, wq), (wk_sb, wk), (wv_sb, wv)):
                sp.dma_start(t[:, :, :], src.rearrange("(k p) n -> p k n", p=P)).then_inc(w_loaded, 16)
            for t, src in ((cos_sb, cos), (sin_sb, sin), (ksin_sb, ksin)):
                sp.dma_start(t[:, :], src).then_inc(w_loaded, 16)
            for c in range(NCHUNK):
                if c >= 2:
                    sp.wait_ge(v_ready, c - 1)
                sp.dma_start(x_ch[:, c % 2], xT[:, c * CH:(c + 1) * CH].rearrange("(k p) t -> p k t", p=P)
                             ).then_inc(x_loaded[c % 2], 16)
            sp.dma_start(wo_sb[:, :, :], wo.rearrange("(k p) n -> p k n", p=P)).then_inc(w3_loaded, 16)
            sp.dma_start(wg_sb[:, :, :], wg.rearrange("(k p) n -> p k n", p=P)).then_inc(w3_loaded, 16)
            sp.dma_start(bg_sb[:, :], bg.rearrange("(a e) -> a e", a=1).to_broadcast([P, E])).then_inc(w3_loaded, 16)

            def load_unit(n, r):
                for g in range(len(QPART)):
                    rows = slice(g * DH, (g + 1) * DH)
                    src = q_parts[QPART[g], :, bass.ds(n * HALF, HALF)].rearrange("a d x h s -> a d (x h s)")
                    sp.dma_start(q_ring[rows, r], src).then_inc(loaded[r], 16)
                    sp.dma_start(k_ring[rows, r], k_parts[KPART[g], :, bass.ds(n * HALF, HALF)]).then_inc(loaded[r], 16)
                sp.dma_start(v_ring[:, r], v_all[:, bass.ds(n * QT * VW, QT * VW)]).then_inc(loaded[r], 16)

            def max_rows(n, r, mt_at, base):
                for half in range(2):
                    sp.wait_ge(sm_free, base + mt_at[half] + 1)
                    dst = q_ring[MROW:MROW + 3, r, half * G * CH:(half + 1) * G * CH].rearrange("k (c t) -> k c t", t=P)
                    sp.dma_start(dst, mt_sb[:, half, :]).then_inc(mrow_set[half], 16)

            for p in range(2):
                sp.wait_ge(stored[p], 16 + NPART * 3)
            sp.wait_ge(v_kept, NCHUNK // 2 + 2)
            for n in range(RING):
                load_unit(n, n)
            max_rows(0, 0, MT_PRO, 0)
            for p in range(2):
                sp.wait_ge(stored[p], 16 + NPART * 6)
            sp.wait_ge(v_kept, NCHUNK + 2)

            def unit(n, r, load):
                max_rows(n + 1, (r + 1) % RING, MT_AT, NPRO + n * NUSE)
                if load:
                    sp.wait_ge(pv_done, n * NSTEP + NSTEP + 3)
                    load_unit(n + RING, r)

            with sp.Fori(0, 4) as i:
                for k in range(RING):
                    unit(i * RING + k, k, True)
            unit(12, 0, True)
            unit(13, 1, False)
            unit(14, 2, False)

            sp.wait_ge(attn_done, 1)
            def load_resid(t, par):
                sp.wait_ge(z_done, t + 1)
                sp.dma_start(x_res[:, par], x[bass.ds(t * P, P), :]).then_inc(xr_loaded[par], 16)

            for par in range(2):
                load_resid(par, par)
            sp.dma_start(we_sb[:, :, :, :], we.rearrange("e (k p) n -> p e k n", p=P)).then_inc(we_loaded, 16)
            with sp.Fori(1, NT // 2) as i:
                for par in range(2):
                    load_resid(i * 2 + par, par)

            sp.wait_ge(a_ready, NT)
            sp.dma_start(be_sb, be.rearrange("(a e) n -> a (e n)", a=1).to_broadcast([P, E * D])).then_inc(we_loaded, 16)
            sp.wait_ge(tab_ready, 1)
            for e in range(E):
                row = sp.value_load(padtab[0:1, e:e + 1], min_val=e * REG, max_val=e * REG + T)
                sp.dma_start(routed[bass.ds(row, P), :], zeros[:, :]).then_inc(padded, 16)
            sp.wait_ge(padded, 16 * E)
            for par in range(2):
                sp.wait_ge(sent[par], 16 * NT)

            def load_tile(k, par):
                sp.wait_ge(xsT_ready, k + 1)
                row = sp.value_load(tab[0:1, 1, bass.ds(k, 1)], min_val=0, max_val=(E - 1) * REG + T)
                sp.dma_start(xs[:, par], routed[bass.ds(row, P), :]).then_inc(xs_loaded[par], 16)

            with sp.Fori(0, TILES // 2) as i:
                for par in range(2):
                    load_tile(i * 2 + par, par)
            load_tile(TILES - 1, 0)

            with sp.Fori(0, NT // 2) as i:
                for par in range(2):
                    t = i * 2 + par
                    sp.wait_ge(y_done, t + 1 + 1)
                    sp.dma_start(out[bass.ds(t * P, P), :], y_out[:, par]).then_inc(y_stored[par], 16)
            for par in range(2):
                sp.wait_ge(y_stored[par], 16 * (NT // 2) + 16)

        @block.gpsimd
        def _(pool):
            pool.memset(ident[:, :], 0.0).then_inc(const_step, 1)
            pool.memset(identb[:, :], 0.0).then_inc(const_step, 1)
            pool.memset(mask[:, :, :], 0.0).then_inc(const_step, 1)
            pool.memset(before[:, :], 1.0).then_inc(const_step, 1)
            pool.wait_ge(const_step, 5)
            for m in (ident, identb):
                pool.affine_select(out=m[:, :], in_=m[:, :], compare_op=ALU.not_equal, fill=1.0, base=0,
                                   pattern=[[-1, P]], channel_multiplier=1).then_inc(const_ready, 1)
            pool.affine_select(out=mask[:, :, :], in_=mask[:, :, :], compare_op=ALU.is_ge, fill=MASKED,
                               base=0, pattern=[[0, G], [-1, P]], channel_multiplier=1).then_inc(const_ready, 1)
            pool.memset(v_all[:, :], 1.0).then_inc(const_ready, 1)
            pool.affine_select(out=before[:, :], in_=before[:, :], compare_op=ALU.is_ge, fill=0.0, base=-1,
                               pattern=[[1, P]], channel_multiplier=-1).then_inc(const_ready, 1)
            pool.iota(eidx[:, :, :], pattern=[[0, 2], [1, E]], base=0, channel_multiplier=0,
                      allow_small_or_imprecise_dtypes=True).then_inc(const_ready, 1)
            pool.iota(eoff[:, :], pattern=[[REG, E]], base=0, channel_multiplier=0,
                      allow_small_or_imprecise_dtypes=True).then_inc(const_ready, 1)
            pool.iota(steps128[:, :, :], pattern=[[0, E], [P, NT]], base=0, channel_multiplier=0,
                      allow_small_or_imprecise_dtypes=True).then_inc(const_ready, 1)
            pool.affine_select(out=upto[:, :, :], in_=upto[:, :, :], compare_op=ALU.is_ge, fill=0.0, base=0,
                               pattern=[[1, E], [-1, E]], channel_multiplier=0).then_inc(const_ready, 1)
            pool.wait_ge(const_ready, 15)
            pool.iota(tnum[:, :, :], pattern=[[1, TILES], [0, E]], base=0, channel_multiplier=0,
                      allow_small_or_imprecise_dtypes=True).then_inc(const_ready, 1)

            with pool.Fori(0, B) as b:
                for u6, p, u in rope_units():
                    U = b * 6 + u6
                    par = u6 % 2
                    pool.wait_ge(rope_mul, U + 1 + 3)
                    pool.wait_ge(part0, U + 1)
                    pool.wait_ge(res0, U + 1)
                    a = rope_t[:, par]
                    if u < 2:
                        pool.tensor_tensor(roped[:, par, 0], a[:, 0], a[:, 1], ALU.subtract)
                        pool.tensor_tensor(roped[:, par, 1], a[:, 2], a[:, 3], ALU.add).then_inc(rope_sum, 1)
                    else:
                        pool.tensor_tensor(roped[:, par, 0], a[:, 0], a[:, 1], ALU.add).then_inc(rope_sum, 1)

            def settle():
                pool.sem_inc(alone, 1)

            def split_max(half, m, seen):
                pool.wait_ge(*seen)
                settle()
                nm = nmax[:, half]
                c = m * 4
                pool.tensor_copy(nparts[:, half, 0:16], nm).then_inc(nsplit, 1)
                pool.wait_ge(nsplit, c + 1)
                pool.tensor_tensor(nres[:, half, 0], nm, nparts[:, half, 0:16], ALU.subtract).then_inc(nsplit, 1)
                pool.wait_ge(nsplit, c + 2)
                settle()
                pool.tensor_copy(nparts[:, half, 16:32], nres[:, half, 0]).then_inc(nsplit, 1)
                pool.wait_ge(nsplit, c + 3)
                pool.tensor_tensor(nres[:, half, 1], nres[:, half, 0], nparts[:, half, 16:32], ALU.subtract
                                   ).then_inc(nsplit, 1)
                pool.wait_ge(nsplit, c + 4)
                settle()
                pool.tensor_copy(nparts[:, half, 32:48], nres[:, half, 1]).then_inc(nparts_ready, 1)

            split_max(0, 0, (sm_free, MX_END[0] + 1))
            split_max(1, 1, (nmax_ready, 1))

            def mask_step(n, s):
                if s in DIAG:
                    pool.wait_ge(exp_done, n * (2 * NSTEP) + 2 * s + 2 + 2)
                    settle()
                    d = probs[:, s % 3, :, 0:P]
                    pool.affine_select(out=d, in_=d, compare_op=ALU.is_ge, fill=0.0, base=0,
                                       pattern=[[0, G], [1, P]], channel_multiplier=-1).then_inc(masked, 1)

            def unit(n, plan, with_max):
                for item in plan:
                    if item[0] == "scores" and item[2] == 1:
                        mask_step(n + item[1] // NSTEP, item[1] % NSTEP)
                    if with_max and item == ("use", MX_END[1]):
                        split_max(0, n * 2 + 2, (sm_free, NPRO + n * NUSE + MX_END[1] + 1))
                    if with_max and item == ("use", MX1_END):
                        split_max(1, n * 2 + 3, (nmax_ready, n + 2))

            mask_step(0, 0)
            mask_step(0, 1)
            with pool.Fori(0, (UNITS - 1) // RING) as i:
                for k in range(RING):
                    unit(i * RING + k, PLAN, True)
            unit(UNITS - 1, PLAN_LAST, False)

            def stage_rows(t, par, sent_before):
                if sent_before is not None:
                    pool.wait_ge(sent[par], sent_before)
                pool.wait_ge(x1_ready, t + 1)
                settle()
                pool.tensor_copy(x1_out[:, par], x1[:, par, :]).then_inc(x1_copied, 1)

            def send_rows(t, par):
                pool.wait_ge(x1_copied, t + 1 + 2)
                pool.wait_ge(pos_ready, t + 1)
                settle()
                for k in range(2):
                    pool.indirect_dma_start(routed[:, :], bass.IndirectOffsetOnAxis(ap=pos[:, par, k:k + 1], axis=0),
                                            x1_out[:, par, :], None).then_inc(sent[par], 16)

            pool.sem_inc(x1_copied, 2)
            stage_rows(0, 0, None)
            stage_rows(1, 1, None)
            send_rows(0, 0)
            with pool.Fori(0, NT // 2 - 1) as i:
                for par in range(2):
                    stage_rows(i * 2 + par + 2, par, i * 32 + 32)
                    send_rows(i * 2 + par + 1, 1 - par)
            send_rows(NT - 1, 1)

            for par in range(2):
                pool.wait_ge(y_sent[par], 16 * ((TILES + 1 - par) // 2) + 16)
            with pool.Fori(0, NT // 2) as i:
                for par in range(2):
                    pool.wait_ge(gpos_ready, i * 2 + par + 1)
                    settle()
                    for k in range(2):
                        pool.indirect_dma_start(got[:, par, k, :], None, experts_out[:, :],
                                                bass.IndirectOffsetOnAxis(ap=gpos[:, par, k:k + 1], axis=0)
                                                ).then_inc(got_rows[par], 16)

        @block.scalar
        def _(act):
            act.sem_inc(part0, 2)
            act.sem_inc(part1, 2)
            for p in range(2):
                act.sem_inc(stored[p], 16)
            act.sem_inc(exp_done, 2)
            act.sem_inc(o_kept, 2)

            def store_parts(b, p, u, par):
                s0 = p * CH
                for k in range(3):
                    for a in range(2):
                        if u < 2:
                            dst = q_parts[k, a, bass.ds(b * 64 + u * 32, 32), p].rearrange("r h s -> h r s")
                            src = parts[:, par, k, a, :]
                        else:
                            dst = k_parts[k, a, bass.ds(b * 64, 64), s0:s0 + CH]
                            src = parts[a * 64:(a + 1) * 64, par, k, 0, :]
                        act.dma_start(dst, src).then_inc(stored[par], 16)

            act.sem_inc(v_kept, 2)
            act.wait_ge(const_ready, 16)
            with act.Fori(0, B) as b:
                for u6, p, u in rope_units():
                    U = b * 6 + u6
                    par = u6 % 2
                    w = 2 if u < 2 else 1
                    act.wait_ge(rope_sum, U + 1 + 2)
                    act.wait_ge(stored[par], (b * 3 + u6 // 2) * NPART + 16)
                    nc.scalar.activation(parts[:, par, 0, 0:w], roped[:, par, 0:w], ACT.Copy).then_inc(part0, 1)
                    if u == 2:
                        act.wait_ge(v_ready, b * 2 + p + 1)
                        dst = v_all[:, bass.ds(b * (HKV * QT * VW), HKV * QT * VW)].rearrange(
                            "p (j t c) -> p t j c", j=HKV, t=QT)[:, 4 * p:4 * p + 4, :, 0:DH]
                        for t in range(4):
                            src = sm[:, p, t * P:(t + 1) * P].rearrange("p (j c) -> p j c", c=DH)
                            ins = nc.scalar.activation(dst[:, t], src, ACT.Copy)
                        ins.then_inc(v_kept, 1)
                    act.wait_ge(res0, U + 1 + 2)
                    nc.scalar.activation(parts[:, par, 1, 0:w], resid[:, par, 0:w], ACT.Copy).then_inc(part1, 1)
                    act.wait_ge(part0, U + 1 + 2)
                    act.wait_ge(part1, U + 1 + 2)
                    act.wait_ge(part2, U + 1)
                    store_parts(b, p, u, par)

            def keep_out(half, n):
                nc.scalar.activation(o_sb[:, half], ot[:, half], ACT.Copy).then_inc(o_kept, 1)

            def weights(n, s):
                w = CH - step_cols(s)
                for hp in range(2):
                    act.wait_ge(st_ready, n * (2 * NSTEP) + 2 * s + hp + 1)
                    act.wait_ge(pv_done, n * NSTEP + s + 1)
                    nc.scalar.activation(probs[:, s % 3, 2 * hp:2 * hp + 2, 0:w], st[:, 2 * hp:2 * hp + 2, 0:w],
                                         ACT.Exp, scale=SCALE).then_inc(exp_done, 1)

            def unit(n, out_at, ahead):
                for s in range(2, NSTEP):
                    weights(n, s)
                    if s == 6:
                        act.wait_ge(pv_done, n * NSTEP + 4 + 3)
                        act.wait_ge(sm_ready, NPRO + n * NUSE - NUSE + OT_A + 1)
                        keep_out(0, n)
                if ahead:
                    weights(n + 1, 0)
                    weights(n + 1, 1)
                act.wait_ge(pv_done, n * NSTEP + NSTEP + 3)
                act.wait_ge(sm_ready, NPRO + n * NUSE + out_at + 1)
                keep_out(1, n)

            weights(0, 0)
            weights(0, 1)
            with act.Fori(0, (UNITS - 1) // RING) as i:
                for k in range(RING):
                    unit(i * RING + k, OT_B, True)
            unit(UNITS - 1, LAST_B, False)

            act.sem_inc(x1_kept, 2)

            def gather_attn(t, par):
                start = CH + (t // QT) * (HKV * CH) + (t % QT) * 64 if isinstance(t, int) else (
                    CH + (t // QT) * (HKV * CH - QT * 64) + t * 64)
                src = attn[:, bass.ds(start, HKV * CH)].rearrange("p (j c) -> p j c", c=CH)
                nc.scalar.activation(a_tok[:, par].rearrange("p (j c) -> p j c", c=64), src[:, :, 0:64], ACT.Copy
                                     ).then_inc(a_ready, 1)

            def turn_attn(t):
                act.wait_ge(trA_ready, t + 1)
                nc.scalar.activation(a_T[:, :, :].rearrange("p k n -> p (k n)"), st[:, 0], ACT.Copy).then_inc(trA_kept, 1)

            def keep_x1(t, par):
                act.wait_ge(trX_ready, t + 1)
                nc.scalar.activation(x_T[:, :, :].rearrange("p k n -> p (k n)"), st[:, 1], ACT.Copy).then_inc(trX_kept, 1)
                nc.scalar.activation(x1_all[:, bass.ds(t * D, D)], x1[:, par], ACT.Copy).then_inc(x1_kept, 1)

            def std(t):
                act.wait_ge(var_ready, t + 1)
                nc.scalar.activation(rstd[:, 0:1], mv[:, 1:2], ACT.Sqrt, bias=eps_sb[:, 0:1]).then_inc(std_ready, 1)

            act.wait_ge(attn_done, 1)
            gather_attn(0, 0)
            gather_attn(1, 1)
            turn_attn(0)
            std(0)
            with act.Fori(0, NT // 2 - 1) as i:
                for par in range(2):
                    t = i * 2 + par
                    turn_attn(t + 1)
                    gather_attn(t + 2, par)
                    keep_x1(t, par)
                    std(t + 1)
            turn_attn(NT - 1)
            keep_x1(NT - 2, 0)
            std(NT - 1)
            keep_x1(NT - 1, 1)

            act.sem_inc(xsT_ready, 2)
            act.sem_inc(e_ready, 2)
            act.sem_inc(yb_done, 2)
            act.sem_inc(yr_done, 2)
            for p in range(2):
                act.sem_inc(y_sent[p], 16)

            def turn_tile(k, par):
                act.wait_ge(xsT_ready, k + 1 + 2)
                act.wait_ge(e_ready, k + 1)
                nc.scalar.activation(xs_T[:, par].rearrange("p k n -> p (k n)"), st[:, par], ACT.Copy).then_inc(xsT_kept, 1)

            def send_tile(k, par):
                act.wait_ge(yb_done, k + 1 + 2)
                act.wait_ge(y_sent[par], (k // 2) * 16 + 16)
                nc.scalar.activation(y_r[:, par], y_b[:, par], ACT.Relu, scale=0.5).then_inc(yr_done, 1)
                act.wait_ge(yr_done, k + 1 + 2)
                act.dma_start(experts_out[bass.ds(k * P, P), :], y_r[:, par]).then_inc(y_sent[par], 16)

            turn_tile(0, 0)
            with act.Fori(0, TILES // 2) as i:
                for par in range(2):
                    turn_tile(i * 2 + par + 1, 1 - par)
                    send_tile(i * 2 + par, par)
            send_tile(TILES - 1, 0)

            with act.Fori(NT, 2 * NT) as t:
                std(t)

        @block.vector
        def _(dve):
            dve.sem_inc(rope_mul, 3)
            dve.sem_inc(rope_sum, 2)
            dve.sem_inc(res0, 2)
            nc.vector.memset(k_ring[MROW:P, :, :], 1.0).then_inc(const_ready, 1)
            nc.vector.memset(o_sb[:, :, :], 1.0).then_inc(const_ready, 1)
            nc.vector.memset(upto[:, :, :], 1.0).then_inc(const_step, 1)
            nc.vector.memset(ones[:, :], 1.0).then_inc(const_ready, 1)
            nc.vector.memset(zeros[:, :], 0.0).then_inc(const_ready, 1)
            nc.vector.memset(sofar[:, :, :], 0.0).then_inc(const_ready, 1)
            nc.vector.memset(eps_sb[:, :], EPS).then_inc(const_ready, 1)

            def products(b, u6, p, u):
                U = b * 6 + u6
                par = u6 % 2
                dve.wait_ge(proj_ready, U + 1)
                dve.wait_ge(rope_sum, U + 1)
                t = rope_t[:, par]
                s0 = p * CH
                c, si, ks = (m[:, s0:s0 + CH] for m in (cos_sb, sin_sb, ksin_sb))
                if u < 2:
                    x1_, x2_ = st[:, 2 * u], st[:, 2 * u + 1]
                    nc.vector.tensor_tensor(t[:, 0], x1_, c, ALU.mult)
                    nc.vector.tensor_tensor(t[:, 1], x2_, si, ALU.mult)
                    nc.vector.tensor_tensor(t[:, 2], x2_, c, ALU.mult)
                    nc.vector.tensor_tensor(t[:, 3], x1_, si, ALU.mult).then_inc(rope_mul, 1)
                else:
                    kk = ot[:, p]
                    nc.vector.tensor_tensor(t[:, 0], kk, c, ALU.mult)
                    nc.vector.tensor_tensor(t[0:64, 1], kk[64:128], ks[64:128], ALU.mult)
                    nc.vector.tensor_tensor(t[64:128, 1], kk[0:64], ks[0:64], ALU.mult).then_inc(rope_mul, 1)

            def residual(b, u6, p, u):
                U = b * 6 + u6
                par, w = u6 % 2, 2 if u < 2 else 1
                dve.wait_ge(part0, U + 1 + 2)
                dve.wait_ge(part1, U + 1)
                nc.vector.tensor_tensor(resid[:, par, 0:w], roped[:, par, 0:w], parts[:, par, 0, 0:w], ALU.subtract
                                        ).then_inc(res0, 1)

            def last_part(b, u6, p, u):
                U = b * 6 + u6
                par, w = u6 % 2, 2 if u < 2 else 1
                dve.wait_ge(part1, U + 1 + 2)
                nc.vector.tensor_tensor(parts[:, par, 2, 0:w], resid[:, par, 0:w], parts[:, par, 1, 0:w], ALU.subtract
                                        ).then_inc(part2, 1)

            dve.wait_ge(w_loaded, 96)
            with dve.Fori(0, B) as b:
                us = rope_units()
                for k in range(len(us) + 2):
                    if k < len(us):
                        products(b, *us[k])
                    if 2 <= k:
                        last_part(b, *us[k - 2])
                    if 1 <= k <= len(us):
                        residual(b, *us[k - 1])

            def reduce_use(half, u, idx_par):
                blocks, chunk = MAXUSES[half][u]
                per, (h0, qt, _, n, _) = len(blocks), blocks[0]
                src = sm[:, idx_par, 0:per * n].rearrange("p (h n) -> p h n", n=n)
                rem = qt % 4
                if half == 0:
                    dst = nmax[:, 0, :].rearrange("p (h q) -> p h q", q=4)[:, h0:h0 + per, rem]
                    return nc.vector.tensor_reduce(dst, src, AX.X, ALU.max, negate=True)
                dst = pmax[:, :, chunk].rearrange("p (h q) -> p h q", q=4)[:, h0:h0 + per, rem]
                return nc.vector.tensor_reduce(dst, src, AX.X, ALU.max)

            def use_banks(n, seq, base, sent, own0):
                outs = 0
                for k, use in enumerate(seq):
                    par = k % 2
                    dve.wait_ge(sm_ready, base + k + 1)
                    if use[0] == "mx":
                        reduce_use(use[1], use[2], par).then_inc(sm_free, 1)
                        if use[1] == 1 and use[2] + 1 == len(MAXUSES[1]):
                            dve.wait_ge(sm_free, base + k + 1)
                            nc.vector.tensor_reduce(nmax[:, 1, :], pmax[:, :, :], AX.X, ALU.max, negate=True
                                                    ).then_inc(nmax_ready, 1)
                    elif use[0] == "mt":
                        if sent is not None:
                            dve.wait_ge(mrow_set[use[1]], sent * 16)
                        bank = sm[:, par].bitcast(BF16)
                        nc.vector.tensor_copy(mt_sb[:, use[1], :], bank[0:48, 0:P]).then_inc(sm_free, 1)
                    else:
                        _, half, back = use
                        slot = (n + 1 - back) * CH + half * 256
                        o_t = sm[:, par].rearrange("p (q c) -> p q c", c=VW)
                        nc.vector.reciprocal(rden[:, half, :], o_t[:, :, DH]).then_inc(dve_own, 1)
                        outs += 1
                        dve.wait_ge(dve_own, own0 + outs)
                        nc.vector.tensor_tensor(attn[:, bass.ds(slot, 256)].rearrange("p (q c) -> p q c", c=DH),
                                                o_t[:, :, 0:DH], rden[:, half, :].unsqueeze(2).to_broadcast([P, 16, DH]),
                                                ALU.mult).then_inc(sm_free, 1)

            dve.wait_ge(v_kept, NCHUNK + 2)
            use_banks(0, PRO, 0, None, 0)
            with dve.Fori(0, (UNITS - 1) // RING) as i:
                for k in range(RING):
                    n = i * RING + k
                    use_banks(n, SEQ, NPRO + n * NUSE, n + 1, n * 2)
            use_banks(UNITS - 1, SEQ_LAST + [("ot", 1, 0)], NPRO + (UNITS - 1) * NUSE, None, (UNITS - 1) * 2)
            dve.wait_ge(sm_free, NPRO + (UNITS - 1) * NUSE + len(SEQ_LAST) + 1)
            dve.sem_inc(attn_done, 1)

            dve.sem_inc(z_done, 2)
            dve.wait_ge(w3_loaded, 48)

            def normed(t, src, dst, own):
                nc.vector.bn_stats(stat[:, :], src).then_inc(own3, 1)
                dve.wait_ge(own3, own + 1)
                dve.sem_inc(alone, 1)
                nc.vector.bn_aggr(mv[:, :], stat[:, :]).then_inc(var_ready, 1)
                dve.wait_ge(std_ready, t + 1)
                nc.vector.reciprocal(rstd[:, 1:2], rstd[:, 0:1]).then_inc(own3, 1)
                dve.wait_ge(own3, own + 2)
                return nc.vector.tensor_scalar(dst, src, mv[:, 0:1], rstd[:, 1:2], ALU.subtract, ALU.mult)

            def norm_tile(t, par, own):
                dve.wait_ge(y_ready, t + 1)
                dve.wait_ge(xr_loaded[par], (t // 2) * 16 + 16)
                if not isinstance(t, int) or t:
                    dve.wait_ge(x1_ready, t)
                nc.vector.tensor_tensor(z[:, :], st[:, 2 + par], x_res[:, par], ALU.add).then_inc(z_done, 1)
                dve.wait_ge(z_done, t + 1 + 2)
                dve.wait_ge(x1_kept, t + 1)
                dve.wait_ge(x1_copied, t + 1)
                normed(t, z[:, :], x1[:, par], own).then_inc(x1_ready, 1)

            def route_tile(t, par, own):
                dve.wait_ge(logit_ready, t + 1)
                nc.vector.tensor_tensor(logit[:, :], ot[:, par, 0:E], bg_sb[:, :], ALU.add).then_inc(own3, 1)
                dve.wait_ge(own3, own + 1)
                dve.sem_inc(alone, 1)
                nc.vector.max(top[:, :], logit[:, :]).then_inc(own3, 1)
                dve.wait_ge(own3, own + 2)
                dve.sem_inc(alone, 1)
                nc.vector.max_index(topi[:, :], top[:, :], logit[:, :]).then_inc(own3, 1)
                dve.wait_ge(own3, own + 3)
                nc.vector.tensor_copy(topf[:, :], topi[:, :]).then_inc(own3, 1)
                dve.wait_ge(own3, own + 4)
                nc.vector.tensor_tensor(hot[:, :, :], eidx[:, :, :], topf[:, 0:2].unsqueeze(2).to_broadcast([P, 2, E]),
                                        ALU.is_equal).then_inc(own3, 1)
                dve.wait_ge(own3, own + 5)
                nc.vector.tensor_tensor(chosen[:, par], hot[:, 0], hot[:, 1], ALU.add).then_inc(chosen_ready, 1)
                dve.wait_ge(chosen_ready, t + 1)
                nc.vector.tensor_tensor(sofar[:, 1 - par], sofar[:, par], chosen[:, par], ALU.add).then_inc(own3, 1)
                dve.wait_ge(rank_ready, t + 1)
                nc.vector.tensor_tensor(rank[:, :], sm[:, par, 0:E], eoff[:, :], ALU.add).then_inc(own3, 1)
                dve.wait_ge(own3, own + 7)
                nc.vector.tensor_tensor(hrank[:, :, :], hot[:, :, :], rank[:, :].unsqueeze(1).to_broadcast([P, 2, E]),
                                        ALU.mult).then_inc(own3, 1)
                dve.wait_ge(own3, own + 8)
                nc.vector.tensor_reduce(posf[:, :], hrank[:, :, :], AX.X, ALU.add).then_inc(own3, 1)
                dve.wait_ge(own3, own + 9)
                dve.wait_ge(x1_copied, t + 1 + 2)
                nc.vector.tensor_copy(pos[:, par], posf[:, :]).then_inc(pos_ready, 1)
                nc.vector.tensor_copy(posf_all[:, bass.ds(t * 2, 2)], posf[:, :])
                nc.vector.tensor_copy(hot_all[:, bass.ds(t * 2, 2)], hot[:, :, :]).then_inc(own3, 1)

            norm_tile(0, 0, 0)
            with dve.Fori(0, NT // 2 - 1) as i:
                for par in range(2):
                    t = i * 2 + par
                    norm_tile(t + 1, 1 - par, t * 12 + 2)
                    route_tile(t, par, t * 12 + 4)
            t = NT - 2
            norm_tile(t + 1, 1, t * 12 + 2)
            route_tile(t, 0, t * 12 + 4)
            route_tile(t + 1, 1, t * 12 + 14)
            own = NT * 12

            def step(ins):
                nonlocal own
                ins.then_inc(own3, 1)
                own += 1
                dve.wait_ge(own3, own)

            dve.wait_ge(count_ready, 1)
            cnt = sm[:, 0, 0:E]
            step(nc.vector.tensor_tensor(padtab[:, :], cnt[0:1], eoff[0:1, :], ALU.add))
            step(nc.vector.tensor_tensor(many[:, :, :], cnt.unsqueeze(2).to_broadcast([P, E, NT]), steps128[:, :, :], ALU.is_gt))
            step(nc.vector.tensor_reduce(ntile[:, :], many[:, :, :], AX.X, ALU.add))
            step(nc.vector.tensor_tensor(cumw[:, :, :], ntile[:, :].unsqueeze(1).to_broadcast([P, E, E]), upto[:, :, :], ALU.mult))
            step(nc.vector.tensor_reduce(cend[:, :], cumw[:, :, :], AX.X, ALU.add))
            step(nc.vector.tensor_tensor(past[:, :, :], cend[0:1, :].unsqueeze(1).to_broadcast([1, TILES, E]), tnum[:, :, :], ALU.is_le))
            step(nc.vector.tensor_reduce(te[:, 0], past[:, :, :], AX.X, ALU.add))
            step(nc.vector.tensor_tensor(pastn[:, :, :], past[:, :, :], ntile[0:1, :].unsqueeze(1).to_broadcast([1, TILES, E]), ALU.mult))
            step(nc.vector.tensor_reduce(te[:, 1], pastn[:, :, :], AX.X, ALU.add))
            step(nc.vector.tensor_scalar(te[:, 2], te[:, 0], float(E), None, ALU.is_lt))
            step(nc.vector.tensor_tensor(te[:, 3], tnum[:, :, 0], te[:, 1], ALU.subtract))
            step(nc.vector.tensor_scalar(te[:, 3], te[:, 3], float(P), None, ALU.mult))
            step(nc.vector.tensor_scalar(te[:, 1], te[:, 0], float(REG), None, ALU.mult))
            step(nc.vector.tensor_tensor(te[:, 3], te[:, 3], te[:, 1], ALU.add))
            step(nc.vector.tensor_tensor(tab[:, 1], te[:, 3], te[:, 2], ALU.mult))
            step(nc.vector.tensor_tensor(tab[:, 0], te[:, 0], te[:, 2], ALU.mult))
            dve.sem_inc(tab_ready, 1)
            step(nc.vector.tensor_tensor(shift[:, :], cend[:, :], ntile[:, :], ALU.subtract))
            step(nc.vector.tensor_scalar(shift[:, :], shift[:, :], float(P), None, ALU.mult))
            step(nc.vector.tensor_tensor(shift[:, :], shift[:, :], eoff[:, :], ALU.subtract))
            step(nc.vector.tensor_tensor(hot_all[:, :, :], hot_all[:, :, :],
                                         shift[:, :].unsqueeze(1).to_broadcast([P, NT * 2, E]), ALU.mult))
            posn = many[:, 0:4].rearrange("p a b -> p (a b)")[:, 0:NT * 2]
            step(nc.vector.tensor_reduce(posn, hot_all[:, :, :], AX.X, ALU.add))
            step(nc.vector.tensor_tensor(posf_all[:, :], posf_all[:, :], posn, ALU.add))
            step(nc.vector.tensor_copy(pos_all[:, :, :].rearrange("p t k -> p (t k)"), posf_all[:, :]))

            dve.wait_ge(we_loaded, 32)

            def add_bias(k, par):
                e = dve.value_load(tab[0:1, 0, bass.ds(k, 1)], min_val=0, max_val=E - 1)
                dve.wait_ge(e_ready, k + 1 + 2)
                dve.wait_ge(yr_done, k + 1)
                nc.vector.tensor_tensor(y_b[:, par], sm[:, par], be_sb[:, bass.ds(e * D, D)], ALU.add).then_inc(yb_done, 1)

            with dve.Fori(0, TILES // 2) as i:
                for par in range(2):
                    add_bias(i * 2 + par, par)
            add_bias(TILES - 1, 0)

            dve.wait_ge(x1_kept, NT + 2)
            dve.sem_inc(summed, 2)
            dve.sem_inc(y_done, 1)
            for p in range(2):
                dve.sem_inc(y_stored[p], 16)

            def rows_of(t, par):
                nc.vector.tensor_copy(gpos[:, par:par + 1], pos_all[:, bass.ds(t, 1)]).then_inc(gpos_ready, 1)

            def finish(t, par):
                o = own + t * 3
                dve.wait_ge(got_rows[par], (t // 2) * 32 + 32)
                dve.wait_ge(y_done, t + 1)
                nc.vector.tensor_tensor(z[:, :], got[:, par, 0], got[:, par, 1], ALU.add).then_inc(own3, 1)
                dve.wait_ge(own3, o + 1)
                nc.vector.tensor_tensor(z[:, :], z[:, :], x1_all[:, bass.ds(t * D, D)], ALU.add).then_inc(summed, 1)
                dve.wait_ge(summed, t + 1 + 2)
                dve.wait_ge(y_stored[par], (t // 2) * 16 + 16)
                normed(t + NT, z[:, :], y_out[:, par], o + 1).then_inc(y_done, 1)

            for par in range(2):
                rows_of(par, par)
            with dve.Fori(0, NT // 2 - 1) as i:
                for par in range(2):
                    finish(i * 2 + par, par)
                    rows_of(i * 2 + par + 2, par)
            for par in range(2):
                finish(NT - 2 + par, par)

        @block.tensor
        def _(pe):
            pe.sem_inc(pv_done, 3)
            pe.wait_ge(w_loaded, 96)
            with pe.Fori(0, B) as b:
                for p in range(2):
                    pe.wait_ge(x_loaded[p], b * 16 + 16)
                    for u in range(3):
                        pe.wait_ge(rope_mul, b * 6 + 3 * p + u + 1)
                        outs = [(st[:, 2 * u + a], wq_sb, (2 * u + a) * P) for a in range(2)] if u < 2 else [(ot[:, p], wk_sb, 0)]
                        for dst, w, col in outs:
                            for k in range(KC):
                                ins = nc.tensor.matmul(dst, w[:, k, col:col + P], x_ch[:, p, k], start=k == 0, stop=k == KC - 1)
                        ins.then_inc(proj_ready, 1)
                    pe.wait_ge(v_kept, b * 2 + p + 1)
                    for t in range(4):
                        for k in range(KC):
                            ins = nc.tensor.matmul(sm[:, p, t * P:(t + 1) * P], x_ch[:, p, k, t * P:(t + 1) * P],
                                                   wv_sb[:, k], start=k == 0, stop=k == KC - 1)
                    ins.then_inc(v_ready, 1)

            def bank_use(use, par, n, r, base_k, halves):
                if not isinstance(base_k, int) or base_k >= 2:
                    pe.wait_ge(sm_free, base_k - 1)
                if use[0] == "mx":
                    blocks, chunk = MAXUSES[use[1]][use[2]]
                    per, m = len(blocks), blocks[0][3]
                    diag = chunk == use[1]
                    if diag:
                        out = sm[:, par, 0:per * m].rearrange("p (h n) -> p h n", n=m)[:, :, m - P:m]
                        nc.tensor.matmul(out, identb[:, :], mask[:, 0:per, :], start=True, stop=False, skip_group_check=True)
                    for h, qt, k0, w, col in blocks:
                        ins = nc.tensor.matmul(sm[:, par, col:col + w], q_ring[0:ROWS, r, q_col(h, qt * P):q_col(h, qt * P) + P],
                                               k_ring[0:ROWS, r, k0:k0 + w], start=not diag, stop=True, skip_group_check=True)
                elif use[0] == "mt":
                    pe.wait_ge(nparts_ready, halves + use[1] + 1)
                    pe.sem_inc(alone, 1)
                    ins = nc.tensor.transpose(sm[:, par].bitcast(BF16)[0:48, 0:P], nparts[:, use[1], :], identb[:, :])
                else:
                    _, half, back = use
                    pe.wait_ge(o_kept, 2 + n * 2 + (0 if back else 1 + half))
                    for q in range(4):
                        ins = nc.tensor.transpose(sm[:, par, q * P:(q + 1) * P], o_sb[:, half, q * P:(q + 1) * P], ident[:, :])
                ins.then_inc(sm_ready, 1)

            def scores(n, r, s, hp):
                half, kb = STEPS[s]
                c0 = step_cols(s)
                if s == 0 and hp == 0:
                    pe.wait_ge(mrow_set[0], n * 16 + 16)
                if s == 4 and hp == 0:
                    pe.wait_ge(mrow_set[1], n * 16 + 16)
                pe.wait_ge(exp_done, n * (2 * NSTEP) + 2 * s + hp + 1)
                for h in (2 * hp, 2 * hp + 1):
                    ins = nc.tensor.matmul(st[:, h, 0:CH - c0], k_ring[0:MROW + 3, r, kb * P:(kb + 1) * P],
                                           q_ring[0:MROW + 3, r, q_col(h, half * CH) + c0:q_col(h, half * CH) + CH],
                                           start=True, stop=True)
                ins.then_inc(st_ready, 1)

            def weigh(n, r, s):
                half, kb = STEPS[s]
                c0 = step_cols(s)
                if kb == 0:
                    pe.wait_ge(o_kept, n * 2 + 1 + half)
                if s in DIAG:
                    pe.wait_ge(masked, n * len(DIAG) + DIAG.index(s) + 1)
                else:
                    pe.wait_ge(exp_done, n * (2 * NSTEP) + 2 * s + 2 + 2)
                last = kb == (3, 7)[half]
                for h in range(G):
                    ins = nc.tensor.matmul(ot[32 * h:32 * h + 32, half, c0:CH], v_ring[:, r, kb * VW:(kb + 1) * VW],
                                           probs[:, s % 3, h, 0:CH - c0], start=kb == 0, stop=last, skip_group_check=True)
                ins.then_inc(pv_done, 1)

            def unit(n, r, seq, plan, next_loads):
                if next_loads is not None:
                    pe.wait_ge(*next_loads)
                for item in plan:
                    if item[0] == "scores":
                        _, s, hp = item
                        scores(n + s // NSTEP, (r + s // NSTEP) % RING, s % NSTEP, hp)
                    elif item[0] == "weigh":
                        weigh(n, r, item[1])
                    else:
                        k = item[1]
                        bank_use(seq[k], k % 2, n, (r + 1) % RING, NPRO + n * NUSE + k, n * 2 + 2)

            pe.wait_ge(const_ready, 16)
            pe.wait_ge(v_kept, NCHUNK + 2)
            pe.wait_ge(loaded[0], LOADS * 16)
            for k, use in enumerate(PRO):
                bank_use(use, k % 2, 0, 0, k, 0)
            pe.wait_ge(rope_mul, NCHUNK * 3 + 3)
            for s in range(2):
                for hp in range(2):
                    scores(0, 0, s, hp)
            with pe.Fori(0, (UNITS - 1) // RING) as i:
                for k in range(RING):
                    unit(i * RING + k, k, SEQ, PLAN,
                         (loaded[(k + 1) % RING], (i + (k + 1) // RING) * (LOADS * 16) + LOADS * 16))
            unit(UNITS - 1, 0, SEQ_LAST, PLAN_LAST, None)
            k = len(SEQ_LAST)
            bank_use(("ot", 1, 0), k % 2, UNITS - 1, 0, NPRO + (UNITS - 1) * NUSE + k, 0)

            pe.wait_ge(w3_loaded, 48)
            pe.wait_ge(attn_done, 1)

            def turn_attn(t, par):
                pe.wait_ge(a_ready, t + 1)
                for k in range(KC):
                    ins = nc.tensor.transpose(st[:, 0, k * P:(k + 1) * P], a_tok[:, par, k * P:(k + 1) * P], ident[:, :])
                ins.then_inc(trA_ready, 1)

            def project(t, par, chunks):
                if 0 in chunks:
                    pe.wait_ge(trA_kept, t + 1)
                    pe.wait_ge(z_done, t + 1)
                for k in chunks:
                    ins = nc.tensor.matmul(st[:, 2 + par], a_T[:, k], wo_sb[:, k], start=k == 0, stop=k == KC - 1)
                if KC - 1 in chunks:
                    ins.then_inc(y_ready, 1)

            def count_before(t, par):
                pe.wait_ge(chosen_ready, t + 1)
                nc.tensor.matmul(sm[:, par, 0:E], before[:, :], chosen[:, par], start=True, stop=False)
                nc.tensor.matmul(sm[:, par, 0:E], ones[:, :], sofar[:, par], start=False, stop=True).then_inc(rank_ready, 1)

            def gate(t, par):
                pe.wait_ge(x1_ready, t + 1)
                for k in range(KC):
                    ins = nc.tensor.transpose(st[:, 1, k * P:(k + 1) * P], x1[:, par, k * P:(k + 1) * P], ident[:, :])
                ins.then_inc(trX_ready, 1)
                pe.wait_ge(trX_kept, t + 1)
                for k in range(KC):
                    ins = nc.tensor.matmul(ot[:, par, 0:E], x_T[:, k], wg_sb[:, k], start=k == 0, stop=k == KC - 1)
                ins.then_inc(logit_ready, 1)

            def tile(t, par, first=False):
                turn_attn(t + 1, 1 - par)
                project(t + 1, 1 - par, (0, 1))
                if not first:
                    count_before(t - 1, 1 - par)
                project(t + 1, 1 - par, (2, 3))
                gate(t, par)

            turn_attn(0, 0)
            project(0, 0, range(KC))
            tile(0, 0, first=True)
            with pe.Fori(0, NT // 2 - 1) as i:
                for k in range(2):
                    tile(i * 2 + k + 1, 1 - k)
            count_before(NT - 2, 0)
            gate(NT - 1, 1)
            count_before(NT - 1, 1)
            pe.wait_ge(own3, NT * 12)
            nc.tensor.matmul(sm[:, 0, 0:E], ones[:, :], sofar[:, 0], start=True, stop=True).then_inc(count_ready, 1)

            pe.wait_ge(we_loaded, 32)
            pe.wait_ge(tab_ready, 1)

            def turn_tile(k, par):
                pe.wait_ge(xs_loaded[par], (k // 2) * 16 + 16)
                for c in range(KC):
                    ins = nc.tensor.transpose(st[:, par, c * P:(c + 1) * P], xs[:, par, c * P:(c + 1) * P], ident[:, :])
                ins.then_inc(xsT_ready, 1)

            def expert(k, par):
                e = pe.value_load(tab[0:1, 0, bass.ds(k, 1)], min_val=0, max_val=E - 1)
                pe.wait_ge(xsT_kept, k + 1)
                pe.wait_ge(yb_done, k + 1)
                for c in range(KC):
                    ins = nc.tensor.matmul(sm[:, par], xs_T[:, par, c], arena[:, bass.ds(e * (KC * D) + c * D, D)],
                                           start=c == 0, stop=c == KC - 1)
                ins.then_inc(e_ready, 1)

            turn_tile(0, 0)
            with pe.Fori(0, TILES // 2) as i:
                for par in range(2):
                    turn_tile(i * 2 + par + 1, 1 - par)
                    expert(i * 2 + par, par)
            expert(TILES - 1, 0)


def kernel(L0_attn_x, L0_attn_Wq, L0_attn_Wk, L0_attn_Wv, L0_attn_Wo, L0_ffn_W_gate, L0_ffn_b_gate, L0_ffn_W_e, L0_ffn_b_e):
    import numpy as np
    import concourse.bacc as bacc
    from concourse.bass_utils import run_bass_kernel_spmd

    x = np.asarray(L0_attn_x).reshape(T, D)
    wq = np.asarray(L0_attn_Wq).reshape(D, 2, 4, G, 2, HALF).transpose(0, 1, 4, 3, 2, 5).reshape(D, D)
    wk = np.asarray(L0_attn_Wk).reshape(D, HKV, 2, HALF).transpose(0, 2, 1, 3).reshape(D, HKV * DH)
    inv = (1.0 / np.float32(10000.0) ** (np.arange(0, DH, 2, dtype=np.float32) / np.float32(DH))).astype(np.float32)
    ang = np.tile((np.arange(S, dtype=np.float32)[:, None] * inv[None, :]).T, (P // HALF, 1))
    cos, sin = np.cos(ang), np.sin(ang)
    ksin = np.where(np.arange(P)[:, None] < 64, sin, -sin)
    data = {
        "xT": x.T, "x": x, "wq": wq, "wk": wk, "wv": L0_attn_Wv, "wo": L0_attn_Wo, "wg": L0_ffn_W_gate,
        "bg": L0_ffn_b_gate, "we": L0_ffn_W_e, "be": L0_ffn_b_e, "cos": cos, "sin": sin, "ksin": ksin,
    }
    nc = bacc.Bacc("TRN2", target_bir_lowering=False, num_devices=1)
    arrays, args = {}, []
    for name, a in data.items():
        a = np.ascontiguousarray(a)
        arrays[name] = a
        args.append(nc.dram_tensor(name, a.shape, mybir.dt.from_np(a.dtype), kind="ExternalInput").ap())
    out = nc.dram_tensor("out", [T, D], F32, kind="ExternalOutput").ap()
    layer(nc, *args, out)
    r = run_bass_kernel_spmd(nc, [arrays], core_ids=[0])
    return np.asarray(r.results[0]["out"]).reshape(B, S, D)
```

```python
from contextlib import ExitStack

import concourse.bass as bass
from concourse import mybir

F32 = mybir.dt.float32
BF16 = mybir.dt.bfloat16
U32 = mybir.dt.uint32
I32 = mybir.dt.int32
ALU = mybir.AluOpType
ACT = mybir.ActivationFunctionType
AX = mybir.AxisListType

P = 128
B, S, D = 2, 1024, 512
T = B * S
HQ, HKV, DH = 32, 8, 16
G = HQ // HKV
HALF = DH // 2
E = 8
KC = D // P
QT = S // P
CH = 512
NCHUNK = T // CH
UNITS = B * HKV
SCALE = DH ** -0.5
EPS = 1e-5
MASKED = -3.0e38
GROUPS = [3, 2, 1]
ROWS = sum(GROUPS) * DH
MROW = ROWS
RING = 3
GOT = 4
LOADS = 2 * len(GROUPS) + 1
STEPS = [(0, kb) for kb in range(4)] + [(1, kb) for kb in range(8)]
NSTEP = len(STEPS)
DIAG = [s for s, (half, kb) in enumerate(STEPS) if kb * P >= half * CH]
TILES = 2 * T // P + E - 1
NT = T // P
REG = T + P
VW = 32


def step_cols(s):
    half, kb = STEPS[s]
    return max(kb * P - half * CH, 0)


def q_col(h, q):
    return (q // CH * G + h) * CH + q % CH


def max_uses():
    uses = [[], []]
    for qt in range(QT):
        half, rem = qt // 4, qt % 4
        if half:
            for h in range(G):
                uses[1].append(([(h, qt, 0, CH, 0)], 0))
        n = (rem + 1) * P
        per = {1: 4, 2: 2, 3: 1, 4: 1}[rem + 1]
        for h0 in range(0, G, per):
            uses[half].append(([(h0 + a, qt, half * CH, n, a * n) for a in range(per)], half))
    return uses


MAXUSES = max_uses()


MX = [("mx", half, u) for half in range(2) for u in range(len(MAXUSES[half]))]

PLAN_STEPS = ["A..W.B.W.", "A..W..B.", "A..B.", "A.W.B.", "A..W.B.W..", "A.B..",
              "A.B.W..", "A.B.W..", "AW..BW", "A.B.", "A.B.W.", "A.B.W"]
PLACES = {4: ("mt", 1), 27: ("mt", 0), 37: ("ot", 1), 38: ("ot", 0)}


def bank_uses(mx, places):
    seq = list(mx)
    for k in sorted(places):
        seq.insert(k, places[k])
    return seq


def body_plan(steps, seq, ahead):
    order, k, weighed = [], 0, 0
    for s, text in enumerate(steps, 2):
        for c in text:
            if c in "AB" and (s < NSTEP or ahead):
                order.append(("scores", s, "AB".index(c)))
            elif c == "W":
                order.append(("weigh", weighed))
                weighed += 1
            elif c == ".":
                order.append(("use", k))
                k += 1
    assert k == len(seq) and weighed == NSTEP
    return order


SEQ = bank_uses(MX, PLACES)
PLAN = body_plan(PLAN_STEPS, SEQ, True)
SEQ_LAST = [("mt", 1), ("ot", 1), ("ot", 0)]
PLAN_LAST = body_plan(["A.BW", "A.BW", "ABW", "ABW", "ABW", "ABW", "ABW."] + ["ABW"] * 5, SEQ_LAST, False)
PRO = bank_uses(MX, {len(MAXUSES[0]) + 3: ("mt", 0)})
NUSE, NPRO = len(SEQ), len(PRO)
assert NUSE % 2 == 0
OT_AT = [SEQ.index(("ot", half)) for half in range(2)]
MT_AT = [SEQ.index(("mt", half)) for half in range(2)]
MX_END = [SEQ.index(("mx", half, len(MAXUSES[half]) - 1)) for half in range(2)]
LAST_OT = SEQ_LAST.index(("ot", 1))
LAST_MT = SEQ_LAST.index(("mt", 1))
PRO_MT = PRO.index(("mt", 0))
PRO_END = PRO.index(("mx", 0, len(MAXUSES[0]) - 1))


def bank(k):
    return (NPRO + k) % 2


def layer(nc, xT, x, wq, wk, wv, wo, wg, bg, we, be, cos, sin, ksin, out):
    ctx = ExitStack()
    with ctx:
        def sb(name, shape, dt):
            return ctx.enter_context(nc.sbuf_tensor(name, shape, dt))

        def sem(name):
            return ctx.enter_context(nc.semaphore(name))

        q_parts = nc.dram_tensor("q_parts", [3, 2, UNITS * HALF, 2, G, CH], BF16, kind="Internal").ap()
        k_parts = nc.dram_tensor("k_parts", [3, UNITS, 2, HALF, S], BF16, kind="Internal").ap()
        routed = nc.dram_tensor("routed", [E * REG, D], F32, kind="Internal").ap()
        experts_out = nc.dram_tensor("experts_out", [TILES * P, D], F32, kind="Internal").ap()

        attn = sb("attn", [P, (UNITS + 1) * CH + P * 4], F32)
        x_ch = attn[:, 0:2 * KC * CH].rearrange("p (b k t) -> p b k t", b=2, k=KC)
        arena = sb("arena", [P, E * KC * D], F32)
        q_ring = arena[:, 0:6144].bitcast(BF16).rearrange("p (r n) -> p r n", r=RING)
        v_all = arena[:, 6144:10240]
        probs = arena[:, 10240:16384].rearrange("p (b h t) -> p b h t", b=3, h=G)
        early = sb("early", [P, 12288], F32)
        wq_sb = early[:, 0:2048].rearrange("p (k n) -> p k n", k=KC)
        wk_sb = early[:, 2048:2560].rearrange("p (k n) -> p k n", k=KC)
        wv_sb = early[:, 2560:3072].rearrange("p (k n) -> p k n", k=KC)
        cos_sb, sin_sb, ksin_sb = (early[:, 3072 + S * i:3072 + S * (i + 1)] for i in range(3))
        resid = early[:, 6144:8192].rearrange("p (b a t) -> p b a t", b=2, a=2)
        parts = early[:, 8192:11264].bitcast(BF16).rearrange("p (b k a t) -> p b k a t", b=2, k=3, a=2)
        x1_all = early[:, 0:NT * D]
        xs = early[:, 8192:9216].rearrange("p (b n) -> p b n", b=2)
        xs_T = early[:, 9216:10240].rearrange("p (b k n) -> p b k n", b=2, k=KC)
        y_b = early[:, 10240:11264].rearrange("p (b n) -> p b n", b=2)
        y_r = early[:, 11264:12288].rearrange("p (b n) -> p b n", b=2)
        be_sb = attn[:, 0:E * D]
        got = attn[:, 4096:8192].rearrange("p (b k n) -> p b k n", b=GOT, k=2)
        y_out = attn[:, 8192:9216].rearrange("p (b n) -> p b n", b=2)
        k_ring = sb("k_ring", [P, RING, S], BF16)
        v_ring = sb("v_ring", [P, RING, QT * VW], F32)
        rope_t = probs[:, 0:2]
        roped = probs[:, 2].rearrange("p (b a) t -> p b a t", b=2)
        ident = sb("ident", [P, P], F32)
        identb = sb("identb", [P, P], BF16)
        mask = sb("mask", [P, G, P], BF16)
        o_sb = sb("o_sb", [P, 2, CH], F32)
        rden = sb("rden", [P, 2, 16], F32)
        pmax = sb("pmax", [P, 16, 2], F32)
        nmax = sb("nmax", [P, 2, 16], F32)
        nres = sb("nres", [P, 2, 2, 16], F32)
        nparts = sb("nparts", [P, 2, 48], BF16)
        mt_sb = sb("mt_sb", [48, 2, P], BF16)
        eps_sb = sb("eps_sb", [P, 1], F32)
        wo_sb = sb("wo_sb", [P, KC, D], F32)
        wg_sb = sb("wg_sb", [P, KC, E], F32)
        bg_sb = sb("bg_sb", [P, E], F32)
        eidx = sb("eidx", [P, 2, E], F32)
        eoff = sb("eoff", [P, E], F32)
        before = sb("before", [P, P], BF16)
        ones = sb("ones", [P, P], BF16)
        zeros = sb("zeros", [P, D], F32)
        a_tok = sb("a_tok", [P, 2, D], F32)
        a_T = sb("a_T", [P, KC, P], F32)
        x_T = sb("x_T", [P, KC, P], F32)
        x_res = sb("x_res", [P, 2, D], F32)
        z = sb("z", [P, 2, D], F32)
        x1 = sb("x1", [P, 2, D], F32)
        x1_out = sb("x1_out", [P, 2, D], F32)
        stat = sb("stat", [P, 2, 6], F32)
        mv = sb("mv", [P, 2, 2], F32)
        rstd = sb("rstd", [P, 2, 2], F32)
        logit = sb("logit", [P, E], F32)
        top = sb("top", [P, 8], F32)
        topi = sb("topi", [P, 8], U32)
        topf = sb("topf", [P, 8], F32)
        hot = sb("hot", [P, 2, E], F32)
        chosen = sb("chosen", [P, 2, E], BF16)
        sofar = sb("sofar", [P, 2, E], BF16)
        rank = sb("rank", [P, E], F32)
        hrank = sb("hrank", [P, 2, E], F32)
        posf = sb("posf", [P, 2], F32)
        pos = sb("pos", [P, 2, 2], U32)
        pos_all = sb("pos_all", [P, NT, 2], U32)
        gpos = sb("gpos", [P, GOT, 2], U32)
        steps128 = sb("steps128", [P, E, NT], F32)
        upto = sb("upto", [P, E, E], F32)
        tnum = sb("tnum", [1, TILES, E], F32)
        many = sb("many", [P, E, NT], F32)
        ntile = sb("ntile", [P, E], F32)
        cumw = sb("cumw", [P, E, E], F32)
        cend = sb("cend", [P, E], F32)
        shift = sb("shift", [P, E], F32)
        hot_all = sb("hot_all", [P, NT * 2, E], F32)
        posf_all = sb("posf_all", [P, NT * 2], F32)
        past = sb("past", [1, TILES, E], F32)
        pastn = sb("pastn", [1, TILES, E], F32)
        te = sb("te", [1, 4, TILES], F32)
        tab = sb("tab", [1, 2, TILES], I32)
        padtab = sb("padtab", [1, E], I32)

        st = ctx.enter_context(nc.psum_tensor("st", [P, G, CH], F32))
        ot = ctx.enter_context(nc.psum_tensor("ot", [P, 2, CH], F32))
        sm = ctx.enter_context(nc.psum_tensor("sm", [P, 2, CH], F32))

        wq_loaded = [sem(f"wq_loaded{u}") for u in range(2)]
        wkv_loaded = sem("wkv_loaded")
        tables_loaded = sem("tables_loaded")
        x_loaded = [sem(f"x_loaded{p}") for p in range(2)]
        proj_ready = sem("proj_ready")
        v_ready = sem("v_ready")
        v_kept = sem("v_kept")
        rope_mul = sem("rope_mul")
        rope_sum = sem("rope_sum")
        part0 = sem("part0")
        res0 = sem("res0")
        part1 = sem("part1")
        part2 = sem("part2")
        stored = [sem(f"stored{p}") for p in range(2)]
        const_ready = sem("const_ready")
        const_step = sem("const_step")
        loaded = [sem(f"loaded{r}") for r in range(RING)]
        sm_ready = sem("sm_ready")
        sm_free = sem("sm_free")
        nmax_ready = sem("nmax_ready")
        nsplit = sem("nsplit")
        nparts_ready = sem("nparts_ready")
        mrow_set = [sem(f"mrow_set{h}") for h in range(2)]
        st_ready = sem("st_ready")
        exp_done = sem("exp_done")
        masked = sem("masked")
        pv_done = sem("pv_done")
        o_kept = sem("o_kept")
        alone = sem("alone")
        dve_own = sem("dve_own")
        attn_done = sem("attn_done")
        w3_loaded = sem("w3_loaded")
        we_loaded = sem("we_loaded")
        a_ready = sem("a_ready")
        trA_ready = sem("trA_ready")
        trA_kept = sem("trA_kept")
        trX_ready = sem("trX_ready")
        trX_kept = sem("trX_kept")
        xr_loaded = [sem(f"xr_loaded{p}") for p in range(2)]
        y_ready = sem("y_ready")
        z_done = sem("z_done")
        own3 = sem("own3")
        var_ready = sem("var_ready")
        std_ready = sem("std_ready")
        rstd_ready = sem("rstd_ready")
        x1_ready = sem("x1_ready")
        x1_kept = sem("x1_kept")
        logit_ready = sem("logit_ready")
        chosen_ready = sem("chosen_ready")
        rank_ready = sem("rank_ready")
        pos_ready = sem("pos_ready")
        sent = [sem(f"sent{p}") for p in range(2)]
        x1_copied = sem("x1_copied")
        count_ready = sem("count_ready")
        padtab_ready = sem("padtab_ready")
        tab_ready = sem("tab_ready")
        padded = sem("padded")
        xs_loaded = [sem(f"xs_loaded{p}") for p in range(2)]
        xsT_ready = sem("xsT_ready")
        xsT_kept = sem("xsT_kept")
        e_ready = sem("e_ready")
        yb_done = sem("yb_done")
        yr_done = sem("yr_done")
        y_sent = [sem(f"y_sent{p}") for p in range(2)]
        gpos_ready = sem("gpos_ready")
        got_rows = [sem(f"got_rows{p}") for p in range(GOT)]
        sum_ready = sem("sum_ready")
        y_done = sem("y_done")
        y_stored = [sem(f"y_stored{p}") for p in range(2)]

        block = ctx.enter_context(nc.Block())

        def stores_of(many):
            return 16 + 6 * 16 * many

        def rope_units():
            return [(3 * p + u, p, u) for p in range(2) for u in range(3)]

        def pad_regions(eng, experts):
            eng.wait_ge(padtab_ready, 1)
            for e in experts:
                row = eng.value_load(padtab[0:1, e:e + 1], min_val=e * REG, max_val=e * REG + T)
                eng.dma_start(routed[bass.ds(row, P), :], zeros[:, :]).then_inc(padded, 16)

        @block.sync
        def _(sp):
            for p in range(2):
                sp.sem_inc(stored[p], 16)
                sp.sem_inc(mrow_set[p], 16)

            def load_chunk(c):
                sp.dma_start(x_ch[:, c % 2], xT[:, c * CH:(c + 1) * CH].rearrange("(k p) t -> p k t", p=P)
                             ).then_inc(x_loaded[c % 2], 16)

            def store_parts(b, u6, p, u):
                par = u6 % 2
                sp.wait_ge(part0, b * 6 + u6 + 1 + 2)
                sp.wait_ge(part1, b * 6 + u6 + 1 + 2)
                sp.wait_ge(part2, b * 6 + u6 + 1)
                for k in range(3):
                    for a in range(2):
                        if u < 2:
                            dst = q_parts[k, a, b * 64 + u * 32:b * 64 + u * 32 + 32, p].rearrange("r h s -> h r s")
                            src = parts[:, par, k, a, :]
                        else:
                            dst = k_parts[k, b * HKV:(b + 1) * HKV, a, :, p * CH:(p + 1) * CH]
                            src = parts[a * 64:(a + 1) * 64, par, k, 0, :]
                        sp.dma_start(dst, src).then_inc(stored[par], 16)

            def load_unit(n, r):
                row = 0
                for j, many_q in enumerate(GROUPS):
                    rows = slice(row, row + many_q * DH)
                    row += many_q * DH
                    src = q_parts[0:many_q, :, bass.ds(n * HALF, HALF)].rearrange("k a d x h s -> (k a) d (x h s)")
                    sp.dma_start(q_ring[rows, r], src).then_inc(loaded[r], 16)
                    src = k_parts[j:j + 1, bass.ds(n, 1)].rearrange("k u a d s -> (k u) (a d) s")
                    sp.dma_start(k_ring[rows, r], src.to_broadcast([many_q, DH, S])).then_inc(loaded[r], 16)
                sp.dma_start(v_ring[:, r], v_all[:, bass.ds(n * QT * VW, QT * VW)]).then_inc(loaded[r], 16)

            def load_weights(t, src, done):
                sp.dma_start(t, src.rearrange("(k p) n -> p k n", p=P)).then_inc(done, 16)

            load_weights(wq_sb[:, :, 0:2 * P], wq[:, 0:2 * P], wq_loaded[0])
            load_chunk(0)
            load_weights(wq_sb[:, :, 2 * P:D], wq[:, 2 * P:D], wq_loaded[1])
            for t, src in ((cos_sb, cos), (sin_sb, sin)):
                sp.dma_start(t[:, :], src).then_inc(tables_loaded, 16)
            load_weights(wk_sb, wk, wkv_loaded)
            load_weights(wv_sb, wv, wkv_loaded)
            sp.dma_start(ksin_sb, ksin).then_inc(tables_loaded, 16)
            load_chunk(1)
            sp.dma_start(wo_sb[:, :, :], wo.rearrange("(k p) n -> p k n", p=P)).then_inc(w3_loaded, 16)
            sp.dma_start(wg_sb[:, :, :], wg.rearrange("(k p) n -> p k n", p=P)).then_inc(w3_loaded, 16)
            sp.dma_start(bg_sb[:, :], bg.rearrange("(a e) -> a e", a=1).to_broadcast([P, E])).then_inc(w3_loaded, 16)

            def max_rows(n, r, half, use):
                sp.wait_ge(sm_free, use + 1)
                dst = q_ring[MROW:MROW + 3, r, half * G * CH:(half + 1) * G * CH].rearrange("k (c t) -> k c t", t=P)
                sp.dma_start(dst, mt_sb[:, half, :]).then_inc(mrow_set[half], 16)

            for c in range(NCHUNK):
                b, p = c // 2, c % 2
                if c == NCHUNK // 2:
                    for q in range(2):
                        sp.wait_ge(stored[q], stores_of(B * 3 // 2))
                    sp.wait_ge(v_kept, NCHUNK // 2 + 2)
                    load_unit(0, 0)
                store_parts(b, 3 * p, p, 0)
                store_parts(b, 3 * p + 1, p, 1)
                if c + 2 < NCHUNK:
                    sp.wait_ge(v_ready, c + 1)
                    load_chunk(c + 2)
                store_parts(b, 3 * p + 2, p, 2)
            load_unit(1, 1)
            max_rows(0, 0, 0, PRO_MT)
            for p in range(2):
                sp.wait_ge(stored[p], stores_of(B * 3))
            sp.wait_ge(v_kept, NCHUNK + 2)

            def unit(n, r, load):
                base = NPRO + n * NUSE
                max_rows(n, r, 1, base + MT_AT[1])
                if load:
                    sp.wait_ge(pv_done, n * NSTEP + 3)
                    load_unit(n + 2, (r + 2) % RING)
                max_rows(n + 1, (r + 1) % RING, 0, base + MT_AT[0])

            with sp.Fori(0, 4) as i:
                for k in range(RING):
                    unit(i * RING + k, k, True)
            unit(12, 0, True)
            unit(13, 1, True)
            unit(14, 2, False)
            max_rows(UNITS - 1, 0, 1, NPRO + (UNITS - 1) * NUSE + LAST_MT)

            def load_resid(t, par, first=False):
                if not first:
                    sp.wait_ge(z_done, t + 1)
                sp.dma_start(x_res[:, par], x[bass.ds(t * P, P), :]).then_inc(xr_loaded[par], 16)

            for par in range(2):
                load_resid(par, par, first=True)
            sp.wait_ge(attn_done, 1)

            def load_expert(e):
                dst = arena[:, bass.ds(e * (KC * D), KC * D)].rearrange("p (k n) -> p k n", k=KC)
                src = we[bass.ds(e, 1)].rearrange("e (k p) n -> p (e k) n", p=P)
                sp.dma_start(dst, src).then_inc(we_loaded, 16)

            load_expert(0)
            def load_pair(i):
                load_expert(i)
                for par in range(2):
                    load_resid(i * 2 + par, par)

            def load_biases(i):
                src = be[bass.ds(i * 2, 2)].rearrange("(a e) n -> a (e n)", a=1).to_broadcast([P, 2 * D])
                sp.dma_start(be_sb[:, bass.ds(i * (2 * D), 2 * D)], src).then_inc(we_loaded, 16)

            with sp.Fori(1, 5) as i:
                load_pair(i)
            sp.wait_ge(a_ready, QT)
            load_biases(0)
            with sp.Fori(5, NT // 2) as i:
                load_pair(i)
                load_biases(i - 4)

            pad_regions(sp, range(0, E // 2))
            sp.wait_ge(padded, 16 * E)
            sp.wait_ge(tab_ready, 1)
            for par in range(2):
                sp.wait_ge(sent[par], 16 * NT)

            def load_tile(k, par):
                sp.wait_ge(xsT_ready, k + 1)
                row = sp.value_load(tab[0:1, 1, bass.ds(k, 1)], min_val=0, max_val=(E - 1) * REG + T)
                sp.dma_start(xs[:, par], routed[bass.ds(row, P), :]).then_inc(xs_loaded[par], 16)

            with sp.Fori(0, TILES // 2) as i:
                for par in range(2):
                    load_tile(i * 2 + par, par)
            load_tile(TILES - 1, 0)

            with sp.Fori(0, NT // 2) as i:
                for par in range(2):
                    t = i * 2 + par
                    sp.wait_ge(y_done, t + 1 + GOT)
                    sp.dma_start(out[bass.ds(t * P, P), :], y_out[:, par]).then_inc(y_stored[par], 16)
            for par in range(2):
                sp.wait_ge(y_stored[par], 16 * (NT // 2) + 16)

        @block.gpsimd
        def _(pool):
            pool.memset(ident[:, :], 0.0).then_inc(const_step, 1)
            pool.memset(identb[:, :], 0.0).then_inc(const_step, 1)
            pool.memset(mask[:, :, :], 0.0).then_inc(const_step, 1)
            pool.memset(before[:, :], 1.0).then_inc(const_step, 1)
            pool.wait_ge(const_step, 5)
            for m in (ident, identb):
                pool.affine_select(out=m[:, :], in_=m[:, :], compare_op=ALU.not_equal, fill=1.0, base=0,
                                   pattern=[[-1, P]], channel_multiplier=1).then_inc(const_ready, 1)
            pool.affine_select(out=mask[:, :, :], in_=mask[:, :, :], compare_op=ALU.is_ge, fill=MASKED,
                               base=0, pattern=[[0, G], [-1, P]], channel_multiplier=1).then_inc(const_ready, 1)
            pool.memset(v_all[:, :], 1.0).then_inc(const_ready, 1)
            pool.affine_select(out=before[:, :], in_=before[:, :], compare_op=ALU.is_ge, fill=0.0, base=-1,
                               pattern=[[1, P]], channel_multiplier=-1).then_inc(const_ready, 1)
            pool.iota(eidx[:, :, :], pattern=[[0, 2], [1, E]], base=0, channel_multiplier=0,
                      allow_small_or_imprecise_dtypes=True).then_inc(const_ready, 1)
            pool.iota(eoff[:, :], pattern=[[REG, E]], base=0, channel_multiplier=0,
                      allow_small_or_imprecise_dtypes=True).then_inc(const_ready, 1)
            pool.iota(steps128[:, :, :], pattern=[[0, E], [P, NT]], base=0, channel_multiplier=0,
                      allow_small_or_imprecise_dtypes=True).then_inc(const_ready, 1)
            pool.affine_select(out=upto[:, :, :], in_=upto[:, :, :], compare_op=ALU.is_ge, fill=0.0, base=0,
                               pattern=[[1, E], [-1, E]], channel_multiplier=0).then_inc(const_ready, 1)
            pool.wait_ge(const_ready, 15)
            pool.iota(tnum[:, :, :], pattern=[[1, TILES], [0, E]], base=0, channel_multiplier=0,
                      allow_small_or_imprecise_dtypes=True).then_inc(const_ready, 1)

            with pool.Fori(0, B) as b:
                for u6, p, u in rope_units():
                    U = b * 6 + u6
                    par = u6 % 2
                    pool.wait_ge(rope_mul, U + 1 + 3)
                    pool.wait_ge(part0, U + 1)
                    pool.wait_ge(res0, U + 1)
                    a = rope_t[:, par]
                    if u < 2:
                        pool.tensor_tensor(roped[:, par, 0], a[:, 0], a[:, 1], ALU.subtract)
                        pool.tensor_tensor(roped[:, par, 1], a[:, 2], a[:, 3], ALU.add).then_inc(rope_sum, 1)
                    else:
                        pool.tensor_tensor(roped[:, par, 0], a[:, 0], a[:, 1], ALU.add).then_inc(rope_sum, 1)

            def settle():
                pool.sem_inc(alone, 1)

            def split_max(half, m, seen):
                pool.wait_ge(*seen)
                settle()
                nm = nmax[:, half]
                c = m * 4
                pool.tensor_copy(nparts[:, half, 0:16], nm).then_inc(nsplit, 1)
                pool.wait_ge(nsplit, c + 1)
                pool.tensor_tensor(nres[:, half, 0], nm, nparts[:, half, 0:16], ALU.subtract).then_inc(nsplit, 1)
                pool.wait_ge(nsplit, c + 2)
                settle()
                pool.tensor_copy(nparts[:, half, 16:32], nres[:, half, 0]).then_inc(nsplit, 1)
                pool.wait_ge(nsplit, c + 3)
                pool.tensor_tensor(nres[:, half, 1], nres[:, half, 0], nparts[:, half, 16:32], ALU.subtract
                                   ).then_inc(nsplit, 1)
                pool.wait_ge(nsplit, c + 4)
                settle()
                pool.tensor_copy(nparts[:, half, 32:48], nres[:, half, 1]).then_inc(nparts_ready, 1)

            split_max(0, 0, (sm_free, PRO_END + 1))

            def mask_step(n, s):
                if s in DIAG:
                    pool.wait_ge(exp_done, n * (2 * NSTEP) + 2 * s + 2 + 2)
                    settle()
                    d = probs[:, s % 3, :, 0:P]
                    pool.affine_select(out=d, in_=d, compare_op=ALU.is_ge, fill=0.0, base=0,
                                       pattern=[[0, G], [1, P]], channel_multiplier=-1).then_inc(masked, 1)

            def unit(n, plan, with_max):
                for item in plan:
                    if item[0] == "scores" and item[2] == 1:
                        mask_step(n + item[1] // NSTEP, item[1] % NSTEP)
                    if with_max and item == ("use", MX_END[0]):
                        split_max(0, n * 2 + 2, (sm_free, NPRO + n * NUSE + MX_END[0] + 1))
                    if with_max and item == ("use", MX_END[1]):
                        split_max(1, n * 2 + 3, (nmax_ready, n + 2))

            mask_step(0, 0)
            mask_step(0, 1)
            split_max(1, 1, (nmax_ready, 1))
            with pool.Fori(0, (UNITS - 1) // RING) as i:
                for k in range(RING):
                    unit(i * RING + k, PLAN, True)
            unit(UNITS - 1, PLAN_LAST, False)

            def stage_rows(t, par, sent_before):
                if sent_before is not None:
                    pool.wait_ge(sent[par], sent_before)
                pool.wait_ge(x1_ready, t + 1)
                settle()
                pool.tensor_copy(x1_out[:, par], x1[:, par, :]).then_inc(x1_copied, 1)

            def send_rows(t, par):
                pool.wait_ge(x1_copied, t + 1 + 2)
                pool.wait_ge(pos_ready, t + 1)
                settle()
                for k in range(2):
                    pool.indirect_dma_start(routed[:, :], bass.IndirectOffsetOnAxis(ap=pos[:, par, k:k + 1], axis=0),
                                            x1_out[:, par, :], None).then_inc(sent[par], 16)

            pool.sem_inc(x1_copied, 2)
            stage_rows(0, 0, None)
            send_rows(0, 0)
            stage_rows(1, 1, None)
            with pool.Fori(0, NT // 2 - 1) as i:
                for par in range(2):
                    send_rows(i * 2 + par + 1, 1 - par)
                    stage_rows(i * 2 + par + 2, par, i * 32 + 32)
            send_rows(NT - 1, 1)

            for par in range(2):
                pool.wait_ge(y_sent[par], 16 * ((TILES + 1 - par) // 2) + 16)
            with pool.Fori(0, NT // GOT) as i:
                for j in range(GOT):
                    pool.wait_ge(gpos_ready, i * GOT + j + 1)
                    settle()
                    for k in range(2):
                        pool.indirect_dma_start(got[:, j, k, :], None, experts_out[:, :],
                                                bass.IndirectOffsetOnAxis(ap=gpos[:, j, k:k + 1], axis=0)
                                                ).then_inc(got_rows[j], 16)

        @block.scalar
        def _(act):
            act.sem_inc(part0, 2)
            act.sem_inc(part1, 2)
            act.sem_inc(exp_done, 2)
            act.sem_inc(o_kept, 2)

            act.sem_inc(v_kept, 2)
            act.wait_ge(const_ready, 16)
            for b in range(B):
                for u6, p, u in rope_units():
                    U = b * 6 + u6
                    par = u6 % 2
                    w = 2 if u < 2 else 1
                    if u == 2:
                        act.wait_ge(v_ready, b * 2 + p + 1)
                        dst = v_all[:, b * (HKV * QT * VW):(b + 1) * (HKV * QT * VW)].rearrange(
                            "p (j t c) -> p t j c", j=HKV, t=QT)[:, 4 * p:4 * p + 4, :, 0:DH]
                        for t in range(4):
                            src = sm[:, p, t * P:(t + 1) * P].rearrange("p (j c) -> p j c", c=DH)
                            ins = nc.scalar.activation(dst[:, t], src, ACT.Copy)
                        ins.then_inc(v_kept, 1)
                    act.wait_ge(rope_sum, U + 1 + 2)
                    act.wait_ge(stored[par], stores_of(U // 2))
                    nc.scalar.activation(parts[:, par, 0, 0:w], roped[:, par, 0:w], ACT.Copy).then_inc(part0, 1)
                    act.wait_ge(res0, U + 1 + 2)
                    nc.scalar.activation(parts[:, par, 1, 0:w], resid[:, par, 0:w], ACT.Copy).then_inc(part1, 1)

            def keep_out(half, n):
                nc.scalar.activation(o_sb[:, half], ot[:, half], ACT.Copy).then_inc(o_kept, 1)

            def weights(n, s):
                w = CH - step_cols(s)
                for hp in range(2):
                    act.wait_ge(st_ready, n * (2 * NSTEP) + 2 * s + hp + 1)
                    act.wait_ge(pv_done, n * NSTEP + s + 1)
                    nc.scalar.activation(probs[:, s % 3, 2 * hp:2 * hp + 2, 0:w], st[:, 2 * hp:2 * hp + 2, 0:w],
                                         ACT.Exp, scale=SCALE).then_inc(exp_done, 1)

            def gather_attn(t, par):
                start = CH + (t // QT) * (HKV * CH) + (t % QT) * 64 if isinstance(t, int) else (
                    CH + (t // QT) * (HKV * CH - QT * 64) + t * 64)
                src = attn[:, bass.ds(start, HKV * CH)].rearrange("p (j c) -> p j c", c=CH)
                nc.scalar.activation(a_tok[:, par].rearrange("p (j c) -> p j c", c=64), src[:, :, 0:64], ACT.Copy
                                     ).then_inc(a_ready, 1)

            def unit(n, out_at, ahead):
                for s in range(2, NSTEP):
                    weights(n, s)
                    if s == 6:
                        act.wait_ge(pv_done, n * NSTEP + 4 + 3)
                        act.wait_ge(sm_ready, NPRO + n * NUSE - NUSE + OT_AT[0] + 1)
                        keep_out(0, n)
                if ahead:
                    weights(n + 1, 0)
                    weights(n + 1, 1)
                else:
                    act.wait_ge(sm_free, NPRO + n * NUSE)
                    gather_attn(0, 0)
                act.wait_ge(pv_done, n * NSTEP + NSTEP + 3)
                act.wait_ge(sm_ready, NPRO + n * NUSE + out_at + 1)
                keep_out(1, n)

            weights(0, 0)
            weights(0, 1)
            with act.Fori(0, (UNITS - 1) // RING) as i:
                for k in range(RING):
                    unit(i * RING + k, OT_AT[1], True)
            unit(UNITS - 1, LAST_OT, False)

            act.sem_inc(x1_kept, 2)

            def turn_attn(t):
                act.wait_ge(trA_ready, t + 1)
                nc.scalar.activation(a_T[:, :, :].rearrange("p k n -> p (k n)"), st[:, 0], ACT.Copy).then_inc(trA_kept, 1)

            def keep_x1_turned(t):
                act.wait_ge(trX_ready, t + 1)
                nc.scalar.activation(x_T[:, :, :].rearrange("p k n -> p (k n)"), st[:, 1], ACT.Copy).then_inc(trX_kept, 1)

            def std(t, par):
                act.wait_ge(var_ready, t + 1)
                nc.scalar.activation(rstd[:, par, 0:1], mv[:, par, 1:2], ACT.Sqrt, bias=eps_sb[:, 0:1]).then_inc(std_ready, 1)

            def keep_x1(t, par):
                nc.scalar.activation(x1_all[:, bass.ds(t * D, D)], x1[:, par], ACT.Copy).then_inc(x1_kept, 1)

            turn_attn(0)
            gather_attn(1, 1)
            act.wait_ge(attn_done, 1)
            gather_attn(2, 0)
            turn_attn(1)
            std(0, 0)
            with act.Fori(0, NT // 2 - 2) as i:
                for par in range(2):
                    t = i * 2 + par
                    keep_x1_turned(t)
                    turn_attn(t + 2)
                    std(t + 1, 1 - par)
                    gather_attn(t + 3, 1 - par)
                    keep_x1(t, par)
            keep_x1_turned(NT - 4)
            turn_attn(NT - 2)
            std(NT - 3, 1)
            gather_attn(NT - 1, 1)
            keep_x1(NT - 4, 0)
            keep_x1_turned(NT - 3)
            turn_attn(NT - 1)
            std(NT - 2, 0)
            keep_x1(NT - 3, 1)
            keep_x1_turned(NT - 2)
            std(NT - 1, 1)
            keep_x1(NT - 2, 0)
            keep_x1_turned(NT - 1)
            keep_x1(NT - 1, 1)

            pad_regions(act, range(E // 2, E))
            act.sem_inc(xsT_ready, 2)
            act.sem_inc(e_ready, 2)
            act.sem_inc(yb_done, 2)
            act.sem_inc(yr_done, 2)
            for p in range(2):
                act.sem_inc(y_sent[p], 16)

            def turn_tile(k, par):
                act.wait_ge(xsT_ready, k + 1 + 2)
                act.wait_ge(e_ready, k + 1)
                nc.scalar.activation(xs_T[:, par].rearrange("p k n -> p (k n)"), st[:, par], ACT.Copy).then_inc(xsT_kept, 1)

            def send_tile(k, par):
                act.wait_ge(yb_done, k + 1 + 2)
                act.wait_ge(y_sent[par], (k // 2) * 16 + 16)
                nc.scalar.activation(y_r[:, par], y_b[:, par], ACT.Relu, scale=0.5).then_inc(yr_done, 1)
                act.wait_ge(yr_done, k + 1 + 2)
                act.dma_start(experts_out[bass.ds(k * P, P), :], y_r[:, par]).then_inc(y_sent[par], 16)

            turn_tile(0, 0)
            with act.Fori(0, TILES // 2) as i:
                for par in range(2):
                    turn_tile(i * 2 + par + 1, 1 - par)
                    send_tile(i * 2 + par, par)
            send_tile(TILES - 1, 0)

            with act.Fori(0, NT // 2) as i:
                for par in range(2):
                    std(i * 2 + par + NT, par)

        @block.vector
        def _(dve):
            dve.sem_inc(rope_mul, 3)
            dve.sem_inc(rope_sum, 2)
            dve.sem_inc(res0, 2)
            nc.vector.memset(k_ring[MROW:P, :, :], 1.0).then_inc(const_ready, 1)
            nc.vector.memset(o_sb[:, :, :], 1.0).then_inc(const_ready, 1)
            nc.vector.memset(upto[:, :, :], 1.0).then_inc(const_step, 1)
            nc.vector.memset(ones[:, :], 1.0).then_inc(const_ready, 1)
            nc.vector.memset(zeros[:, :], 0.0).then_inc(const_ready, 1)
            nc.vector.memset(sofar[:, :, :], 0.0).then_inc(const_ready, 1)
            nc.vector.memset(eps_sb[:, :], EPS).then_inc(const_ready, 1)

            def products(b, u6, p, u):
                U = b * 6 + u6
                par = u6 % 2
                dve.wait_ge(proj_ready, U + 1)
                dve.wait_ge(rope_sum, U + 1)
                t = rope_t[:, par]
                s0 = p * CH
                c, si, ks = (m[:, s0:s0 + CH] for m in (cos_sb, sin_sb, ksin_sb))
                if u < 2:
                    x1_, x2_ = st[:, 2 * u], st[:, 2 * u + 1]
                    nc.vector.tensor_tensor(t[:, 0], x1_, c, ALU.mult)
                    nc.vector.tensor_tensor(t[:, 1], x2_, si, ALU.mult)
                    nc.vector.tensor_tensor(t[:, 2], x2_, c, ALU.mult)
                    nc.vector.tensor_tensor(t[:, 3], x1_, si, ALU.mult).then_inc(rope_mul, 1)
                else:
                    kk = ot[:, p]
                    nc.vector.tensor_tensor(t[:, 0], kk, c, ALU.mult)
                    nc.vector.tensor_tensor(t[0:64, 1], kk[64:128], ks[64:128], ALU.mult)
                    nc.vector.tensor_tensor(t[64:128, 1], kk[0:64], ks[0:64], ALU.mult).then_inc(rope_mul, 1)

            def residual(b, u6, p, u):
                U = b * 6 + u6
                par, w = u6 % 2, 2 if u < 2 else 1
                dve.wait_ge(part0, U + 1 + 2)
                dve.wait_ge(part1, U + 1)
                nc.vector.tensor_tensor(resid[:, par, 0:w], roped[:, par, 0:w], parts[:, par, 0, 0:w], ALU.subtract
                                        ).then_inc(res0, 1)

            def last_part(b, u6, p, u):
                U = b * 6 + u6
                par, w = u6 % 2, 2 if u < 2 else 1
                dve.wait_ge(part1, U + 1 + 2)
                nc.vector.tensor_tensor(parts[:, par, 2, 0:w], resid[:, par, 0:w], parts[:, par, 1, 0:w], ALU.subtract
                                        ).then_inc(part2, 1)

            dve.wait_ge(tables_loaded, 48)
            us = [(b, *u) for b in range(B) for u in rope_units()]
            for k in range(len(us)):
                products(*us[k])
                if 2 <= k:
                    last_part(*us[k - 2])
                if 1 <= k:
                    residual(*us[k - 1])

            def reduce_use(half, u, idx_par):
                blocks, chunk = MAXUSES[half][u]
                per, (h0, qt, _, n, _) = len(blocks), blocks[0]
                src = sm[:, idx_par, 0:per * n].rearrange("p (h n) -> p h n", n=n)
                rem = qt % 4
                if half == 0:
                    dst = nmax[:, 0, :].rearrange("p (h q) -> p h q", q=4)[:, h0:h0 + per, rem]
                    return nc.vector.tensor_reduce(dst, src, AX.X, ALU.max, negate=True)
                dst = pmax[:, :, chunk].rearrange("p (h q) -> p h q", q=4)[:, h0:h0 + per, rem]
                return nc.vector.tensor_reduce(dst, src, AX.X, ALU.max)

            def use_banks(n, seq, base, base_par, own0, back=True, between={}):
                outs = 0
                for k, use in enumerate(seq):
                    for piece, unit_of in between.get(k, ()):
                        piece(*unit_of)
                    par = (base_par + k) % 2
                    dve.wait_ge(sm_ready, base + k + 1)
                    if use[0] == "mx":
                        reduce_use(use[1], use[2], par).then_inc(sm_free, 1)
                        if use[1] == 1 and use[2] + 1 == len(MAXUSES[1]):
                            dve.wait_ge(sm_free, base + k + 1)
                            nc.vector.tensor_reduce(nmax[:, 1, :], pmax[:, :, :], AX.X, ALU.max, negate=True
                                                    ).then_inc(nmax_ready, 1)
                    elif use[0] == "mt":
                        dve.wait_ge(mrow_set[use[1]], 16 if base_par == 0 else n * 16 + (16 if use[1] else 32))
                        bank = sm[:, par].bitcast(BF16)
                        nc.vector.tensor_copy(mt_sb[:, use[1], :], bank[0:48, 0:P]).then_inc(sm_free, 1)
                    else:
                        half = use[1]
                        slot = (n + 1 - (half if back else 0)) * CH + half * 256
                        o_t = sm[:, par].rearrange("p (q c) -> p q c", c=VW)
                        nc.vector.reciprocal(rden[:, half, :], o_t[:, :, DH]).then_inc(dve_own, 1)
                        outs += 1
                        dve.wait_ge(dve_own, own0 + outs)
                        nc.vector.tensor_tensor(attn[:, bass.ds(slot, 256)].rearrange("p (q c) -> p q c", c=DH),
                                                o_t[:, :, 0:DH], rden[:, half, :].unsqueeze(2).to_broadcast([P, 16, DH]),
                                                ALU.mult).then_inc(sm_free, 1)

            use_banks(0, PRO, 0, 0, 0, between={4: [(last_part, us[-2]), (residual, us[-1])], 9: [(last_part, us[-1])]})
            with dve.Fori(0, (UNITS - 1) // RING) as i:
                for k in range(RING):
                    n = i * RING + k
                    use_banks(n, SEQ, NPRO + n * NUSE, NPRO, n * 2)
            base = NPRO + (UNITS - 1) * NUSE
            use_banks(UNITS - 1, SEQ_LAST, base, NPRO, (UNITS - 1) * 2)
            use_banks(UNITS - 1, [("ot", 1)], base + len(SEQ_LAST), NPRO + len(SEQ_LAST), UNITS * 2, back=False)
            dve.wait_ge(sm_free, NPRO + (UNITS - 1) * NUSE + len(SEQ_LAST) + 1)
            dve.sem_inc(attn_done, 1)

            dve.sem_inc(z_done, 2)
            dve.wait_ge(w3_loaded, 48)

            def moments(t, par, src, own):
                nc.vector.bn_stats(stat[:, par], src).then_inc(own3, 1)
                dve.wait_ge(own3, own + 1)
                dve.sem_inc(alone, 1)
                nc.vector.bn_aggr(mv[:, par], stat[:, par]).then_inc(var_ready, 1)

            def normed(t, par, src, dst):
                dve.wait_ge(std_ready, t + 1)
                nc.vector.reciprocal(rstd[:, par, 1:2], rstd[:, par, 0:1]).then_inc(rstd_ready, 1)
                dve.wait_ge(rstd_ready, t + 1)
                return nc.vector.tensor_scalar(dst, src, mv[:, par, 0:1], rstd[:, par, 1:2], ALU.subtract, ALU.mult)

            def norm_tile(t, par, own):
                dve.wait_ge(y_ready, t + 1)
                dve.wait_ge(xr_loaded[par], (t // 2) * 16 + 16)
                nc.vector.tensor_tensor(z[:, par], st[:, 2 + par], x_res[:, par], ALU.add).then_inc(z_done, 1)
                dve.wait_ge(z_done, t + 1 + 2)
                moments(t, par, z[:, par], own)
                dve.wait_ge(x1_kept, t + 1)
                dve.wait_ge(x1_copied, t + 1)
                normed(t, par, z[:, par], x1[:, par]).then_inc(x1_ready, 1)

            def route_tile(t, par, own):
                dve.wait_ge(logit_ready, t + 1)
                nc.vector.tensor_tensor(logit[:, :], ot[:, par, 0:E], bg_sb[:, :], ALU.add).then_inc(own3, 1)
                dve.wait_ge(own3, own + 1)
                dve.sem_inc(alone, 1)
                nc.vector.max(top[:, :], logit[:, :]).then_inc(own3, 1)
                dve.wait_ge(own3, own + 2)
                dve.sem_inc(alone, 1)
                nc.vector.max_index(topi[:, :], top[:, :], logit[:, :]).then_inc(own3, 1)
                dve.wait_ge(own3, own + 3)
                nc.vector.tensor_copy(topf[:, :], topi[:, :]).then_inc(own3, 1)
                dve.wait_ge(own3, own + 4)
                nc.vector.tensor_tensor(hot[:, :, :], eidx[:, :, :], topf[:, 0:2].unsqueeze(2).to_broadcast([P, 2, E]),
                                        ALU.is_equal).then_inc(own3, 1)
                dve.wait_ge(own3, own + 5)
                nc.vector.tensor_tensor(chosen[:, par], hot[:, 0], hot[:, 1], ALU.add).then_inc(chosen_ready, 1)
                dve.wait_ge(chosen_ready, t + 1)
                nc.vector.tensor_tensor(sofar[:, 1 - par], sofar[:, par], chosen[:, par], ALU.add).then_inc(own3, 1)
                dve.wait_ge(rank_ready, t + 1)
                nc.vector.tensor_tensor(rank[:, :], sm[:, par, 0:E], eoff[:, :], ALU.add).then_inc(own3, 1)
                dve.wait_ge(own3, own + 7)
                nc.vector.tensor_tensor(hrank[:, :, :], hot[:, :, :], rank[:, :].unsqueeze(1).to_broadcast([P, 2, E]),
                                        ALU.mult).then_inc(own3, 1)
                dve.wait_ge(own3, own + 8)
                nc.vector.tensor_reduce(posf[:, :], hrank[:, :, :], AX.X, ALU.add).then_inc(own3, 1)
                dve.wait_ge(own3, own + 9)
                dve.wait_ge(x1_copied, t + 1 + 2)
                nc.vector.tensor_copy(pos[:, par], posf[:, :]).then_inc(pos_ready, 1)
                nc.vector.tensor_copy(posf_all[:, bass.ds(t * 2, 2)], posf[:, :])
                nc.vector.tensor_copy(hot_all[:, bass.ds(t * 2, 2)], hot[:, :, :]).then_inc(own3, 1)

            norm_tile(0, 0, 0)
            with dve.Fori(0, NT // 2 - 1) as i:
                for par in range(2):
                    t = i * 2 + par
                    norm_tile(t + 1, 1 - par, t * 11 + 1)
                    route_tile(t, par, t * 11 + 2)
            t = NT - 2
            norm_tile(t + 1, 1, t * 11 + 1)
            route_tile(t, 0, t * 11 + 2)
            route_tile(t + 1, 1, t * 11 + 12)
            own = NT * 11

            def step(ins):
                nonlocal own
                ins.then_inc(own3, 1)
                own += 1
                dve.wait_ge(own3, own)

            dve.wait_ge(count_ready, 1)
            cnt = sm[:, 0, 0:E]
            step(nc.vector.tensor_tensor(padtab[:, :], cnt[0:1], eoff[0:1, :], ALU.add))
            dve.sem_inc(padtab_ready, 1)
            step(nc.vector.tensor_tensor(many[:, :, :], cnt.unsqueeze(2).to_broadcast([P, E, NT]), steps128[:, :, :], ALU.is_gt))
            step(nc.vector.tensor_reduce(ntile[:, :], many[:, :, :], AX.X, ALU.add))
            step(nc.vector.tensor_tensor(cumw[:, :, :], ntile[:, :].unsqueeze(1).to_broadcast([P, E, E]), upto[:, :, :], ALU.mult))
            step(nc.vector.tensor_reduce(cend[:, :], cumw[:, :, :], AX.X, ALU.add))
            step(nc.vector.tensor_tensor(past[:, :, :], cend[0:1, :].unsqueeze(1).to_broadcast([1, TILES, E]), tnum[:, :, :], ALU.is_le))
            step(nc.vector.tensor_reduce(te[:, 0], past[:, :, :], AX.X, ALU.add))
            step(nc.vector.tensor_tensor(pastn[:, :, :], past[:, :, :], ntile[0:1, :].unsqueeze(1).to_broadcast([1, TILES, E]), ALU.mult))
            step(nc.vector.tensor_reduce(te[:, 1], pastn[:, :, :], AX.X, ALU.add))
            step(nc.vector.tensor_scalar(te[:, 2], te[:, 0], float(E), None, ALU.is_lt))
            step(nc.vector.tensor_tensor(te[:, 3], tnum[:, :, 0], te[:, 1], ALU.subtract))
            step(nc.vector.tensor_scalar(te[:, 3], te[:, 3], float(P), None, ALU.mult))
            step(nc.vector.tensor_scalar(te[:, 1], te[:, 0], float(REG), None, ALU.mult))
            step(nc.vector.tensor_tensor(te[:, 3], te[:, 3], te[:, 1], ALU.add))
            step(nc.vector.tensor_tensor(tab[:, 1], te[:, 3], te[:, 2], ALU.mult))
            step(nc.vector.tensor_tensor(tab[:, 0], te[:, 0], te[:, 2], ALU.mult))
            dve.sem_inc(tab_ready, 1)
            step(nc.vector.tensor_tensor(shift[:, :], cend[:, :], ntile[:, :], ALU.subtract))
            step(nc.vector.tensor_scalar(shift[:, :], shift[:, :], float(P), None, ALU.mult))
            step(nc.vector.tensor_tensor(shift[:, :], shift[:, :], eoff[:, :], ALU.subtract))
            step(nc.vector.tensor_tensor(hot_all[:, :, :], hot_all[:, :, :],
                                         shift[:, :].unsqueeze(1).to_broadcast([P, NT * 2, E]), ALU.mult))
            posn = many[:, 0:4].rearrange("p a b -> p (a b)")[:, 0:NT * 2]
            step(nc.vector.tensor_reduce(posn, hot_all[:, :, :], AX.X, ALU.add))
            step(nc.vector.tensor_tensor(posf_all[:, :], posf_all[:, :], posn, ALU.add))
            step(nc.vector.tensor_copy(pos_all[:, :, :].rearrange("p t k -> p (t k)"), posf_all[:, :]))

            dve.wait_ge(we_loaded, 16 * (E + E // 2))

            def add_bias(k, par):
                e = dve.value_load(tab[0:1, 0, bass.ds(k, 1)], min_val=0, max_val=E - 1)
                dve.wait_ge(e_ready, k + 1 + 2)
                dve.wait_ge(yr_done, k + 1)
                nc.vector.tensor_tensor(y_b[:, par], sm[:, par], be_sb[:, bass.ds(e * D, D)], ALU.add).then_inc(yb_done, 1)

            with dve.Fori(0, TILES // 2) as i:
                for par in range(2):
                    add_bias(i * 2 + par, par)
            add_bias(TILES - 1, 0)

            dve.wait_ge(x1_kept, NT + 2)
            dve.sem_inc(y_done, GOT)
            for p in range(2):
                dve.sem_inc(y_stored[p], 16)

            def rows_of(t, j):
                nc.vector.tensor_copy(gpos[:, j:j + 1], pos_all[:, bass.ds(t, 1)]).then_inc(gpos_ready, 1)

            def measure(t, j, own):
                dve.wait_ge(sum_ready, t + 1)
                moments(t + NT, j % 2, st[:, j], own)

            def finish(t, j):
                par = j % 2
                dve.wait_ge(y_stored[par], (t // 2) * 16 + 16)
                normed(t + NT, par, st[:, j], y_out[:, par]).then_inc(y_done, 1)

            for j in range(GOT):
                rows_of(j, j)
            measure(0, 0, own)
            with dve.Fori(0, NT // GOT - 1) as i:
                for j in range(GOT):
                    t = i * GOT + j
                    rows_of(t + GOT, j)
                    measure(t + 1, (j + 1) % GOT, own + t + 1)
                    finish(t, j)
            for t in range(NT - GOT, NT - 1):
                measure(t + 1, (t + 1) % GOT, own + t + 1)
                finish(t, t % GOT)
            finish(NT - 1, GOT - 1)

        @block.tensor
        def _(pe):
            pe.sem_inc(pv_done, 3)
            pe.wait_ge(wq_loaded[0], 16)
            with pe.Fori(0, B) as b:
                for p in range(2):
                    pe.wait_ge(x_loaded[p], b * 16 + 16)
                    for u in range(3):
                        pe.wait_ge(rope_mul, b * 6 + 3 * p + u + 1)
                        if p == 0 and u == 1:
                            pe.wait_ge(wq_loaded[1], 16)
                        if p == 0 and u == 2:
                            pe.wait_ge(wkv_loaded, 32)
                        outs = [(st[:, 2 * u + a], wq_sb, (2 * u + a) * P) for a in range(2)] if u < 2 else [(ot[:, p], wk_sb, 0)]
                        for dst, w, col in outs:
                            for k in range(KC):
                                ins = nc.tensor.matmul(dst, w[:, k, col:col + P], x_ch[:, p, k], start=k == 0, stop=k == KC - 1)
                        ins.then_inc(proj_ready, 1)
                    pe.wait_ge(v_kept, b * 2 + p + 1)
                    for t in range(4):
                        for k in range(KC):
                            ins = nc.tensor.matmul(sm[:, p, t * P:(t + 1) * P], x_ch[:, p, k, t * P:(t + 1) * P],
                                                   wv_sb[:, k], start=k == 0, stop=k == KC - 1)
                    ins.then_inc(v_ready, 1)

            def bank_use(use, par, n, r, base_k, halves, back=True):
                if not isinstance(base_k, int) or base_k >= 2:
                    pe.wait_ge(sm_free, base_k - 1)
                if use[0] == "mx":
                    blocks, chunk = MAXUSES[use[1]][use[2]]
                    per, m = len(blocks), blocks[0][3]
                    diag = chunk == use[1]
                    if diag:
                        out = sm[:, par, 0:per * m].rearrange("p (h n) -> p h n", n=m)[:, :, m - P:m]
                        nc.tensor.matmul(out, identb[:, :], mask[:, 0:per, :], start=True, stop=False, skip_group_check=True)
                    for h, qt, k0, w, col in blocks:
                        ins = nc.tensor.matmul(sm[:, par, col:col + w], q_ring[0:ROWS, r, q_col(h, qt * P):q_col(h, qt * P) + P],
                                               k_ring[0:ROWS, r, k0:k0 + w], start=not diag, stop=True, skip_group_check=True)
                elif use[0] == "mt":
                    pe.wait_ge(nparts_ready, halves)
                    pe.sem_inc(alone, 1)
                    ins = nc.tensor.transpose(sm[:, par].bitcast(BF16)[0:48, 0:P], nparts[:, use[1], :], identb[:, :])
                else:
                    half = use[1]
                    pe.wait_ge(o_kept, 2 + n * 2 + (1 - half if back else 2))
                    for q in range(4):
                        ins = nc.tensor.transpose(sm[:, par, q * P:(q + 1) * P], o_sb[:, half, q * P:(q + 1) * P], ident[:, :])
                ins.then_inc(sm_ready, 1)

            def scores(n, r, s, hp):
                half, kb = STEPS[s]
                c0 = step_cols(s)
                if s == 0 and hp == 0:
                    pe.wait_ge(mrow_set[0], n * 16 + 32)
                if s == 4 and hp == 0:
                    pe.wait_ge(mrow_set[1], n * 16 + 32)
                pe.wait_ge(exp_done, n * (2 * NSTEP) + 2 * s + hp + 1)
                for h in (2 * hp, 2 * hp + 1):
                    ins = nc.tensor.matmul(st[:, h, 0:CH - c0], k_ring[0:MROW + 3, r, kb * P:(kb + 1) * P],
                                           q_ring[0:MROW + 3, r, q_col(h, half * CH) + c0:q_col(h, half * CH) + CH],
                                           start=True, stop=True)
                ins.then_inc(st_ready, 1)

            def weigh(n, r, s):
                half, kb = STEPS[s]
                c0 = step_cols(s)
                if kb == 0:
                    pe.wait_ge(o_kept, n * 2 + 1 + half)
                if s in DIAG:
                    pe.wait_ge(masked, n * len(DIAG) + DIAG.index(s) + 1)
                else:
                    pe.wait_ge(exp_done, n * (2 * NSTEP) + 2 * s + 2 + 2)
                last = kb == (3, 7)[half]
                for h in range(G):
                    ins = nc.tensor.matmul(ot[32 * h:32 * h + 32, half, c0:CH], v_ring[:, r, kb * VW:(kb + 1) * VW],
                                           probs[:, s % 3, h, 0:CH - c0], start=kb == 0, stop=last, skip_group_check=True)
                ins.then_inc(pv_done, 1)

            def unit(n, r, seq, plan, next_loads):
                if next_loads is not None:
                    pe.wait_ge(*next_loads)
                for item in plan:
                    if item[0] == "scores":
                        _, s, hp = item
                        scores(n + s // NSTEP, (r + s // NSTEP) % RING, s % NSTEP, hp)
                    elif item[0] == "weigh":
                        weigh(n, r, item[1])
                    else:
                        k = item[1]
                        bank_use(seq[k], bank(k), n, (r + 1) % RING, NPRO + n * NUSE + k, n * 2 + 3 - seq[k][1])

            pe.wait_ge(const_ready, 16)
            pe.wait_ge(v_kept, NCHUNK + 2)
            pe.wait_ge(loaded[0], LOADS * 16)
            for k, use in enumerate(PRO):
                bank_use(use, k % 2, 0, 0, k, 1)
                if NPRO - 8 <= k < NPRO - 4:
                    if k == NPRO - 8:
                        pe.wait_ge(rope_mul, NCHUNK * 3 + 3)
                    scores(0, 0, (k - NPRO + 8) // 2, (k - NPRO + 8) % 2)
            with pe.Fori(0, (UNITS - 1) // RING) as i:
                for k in range(RING):
                    unit(i * RING + k, k, SEQ, PLAN,
                         (loaded[(k + 1) % RING], (i + (k + 1) // RING) * (LOADS * 16) + LOADS * 16))
            unit(UNITS - 1, 0, SEQ_LAST, PLAN_LAST, None)

            def turn_attn(t, par):
                pe.wait_ge(a_ready, t + 1)
                for k in range(KC):
                    ins = nc.tensor.transpose(st[:, 0, k * P:(k + 1) * P], a_tok[:, par, k * P:(k + 1) * P], ident[:, :])
                ins.then_inc(trA_ready, 1)

            turn_attn(0, 0)
            k = len(SEQ_LAST)
            bank_use(("ot", 1), bank(k), UNITS - 1, 0, NPRO + (UNITS - 1) * NUSE + k, 0, back=False)

            pe.wait_ge(w3_loaded, 48)

            def project(t, par, chunks):
                if 0 in chunks:
                    pe.wait_ge(trA_kept, t + 1)
                    pe.wait_ge(z_done, t + 1)
                for k in chunks:
                    ins = nc.tensor.matmul(st[:, 2 + par], a_T[:, k], wo_sb[:, k], start=k == 0, stop=k == KC - 1)
                if KC - 1 in chunks:
                    ins.then_inc(y_ready, 1)

            def count_before(t, par):
                pe.wait_ge(chosen_ready, t + 1)
                nc.tensor.matmul(sm[:, par, 0:E], before[:, :], chosen[:, par], start=True, stop=False)
                nc.tensor.matmul(sm[:, par, 0:E], ones[:, :], sofar[:, par], start=False, stop=True).then_inc(rank_ready, 1)

            def turn_x1(t, par):
                pe.wait_ge(x1_ready, t + 1)
                for k in range(KC):
                    ins = nc.tensor.transpose(st[:, 1, k * P:(k + 1) * P], x1[:, par, k * P:(k + 1) * P], ident[:, :])
                ins.then_inc(trX_ready, 1)

            def gate(t, par):
                pe.wait_ge(trX_kept, t + 1)
                for k in range(KC):
                    ins = nc.tensor.matmul(ot[:, par, 0:E], x_T[:, k], wg_sb[:, k], start=k == 0, stop=k == KC - 1)
                ins.then_inc(logit_ready, 1)

            def tile(t, par, first=False, more=True):
                project(t + 1, 1 - par, (0, 1, 2))
                if not first:
                    count_before(t - 1, 1 - par)
                project(t + 1, 1 - par, (3,))
                turn_x1(t, par)
                if more:
                    turn_attn(t + 2, par)
                gate(t, par)

            project(0, 0, range(KC))
            pe.wait_ge(attn_done, 1)
            turn_attn(1, 1)
            tile(0, 0, first=True)
            with pe.Fori(0, NT // 2 - 2) as i:
                for k in range(2):
                    tile(i * 2 + k + 1, 1 - k)
            tile(NT - 3, 1)
            tile(NT - 2, 0, more=False)
            count_before(NT - 2, 0)
            turn_x1(NT - 1, 1)
            gate(NT - 1, 1)
            count_before(NT - 1, 1)
            pe.wait_ge(own3, NT * 11)
            nc.tensor.matmul(sm[:, 0, 0:E], ones[:, :], sofar[:, 0], start=True, stop=True).then_inc(count_ready, 1)

            pe.wait_ge(we_loaded, 16 * (E + E // 2))
            pe.wait_ge(tab_ready, 1)

            def turn_tile(k, par):
                pe.wait_ge(xs_loaded[par], (k // 2) * 16 + 16)
                for c in range(KC):
                    ins = nc.tensor.transpose(st[:, par, c * P:(c + 1) * P], xs[:, par, c * P:(c + 1) * P], ident[:, :])
                ins.then_inc(xsT_ready, 1)

            def expert(k, par):
                e = pe.value_load(tab[0:1, 0, bass.ds(k, 1)], min_val=0, max_val=E - 1)
                pe.wait_ge(xsT_kept, k + 1)
                pe.wait_ge(yb_done, k + 1)
                for c in range(KC):
                    ins = nc.tensor.matmul(sm[:, par], xs_T[:, par, c], arena[:, bass.ds(e * (KC * D) + c * D, D)],
                                           start=c == 0, stop=c == KC - 1)
                ins.then_inc(e_ready, 1)

            turn_tile(0, 0)
            with pe.Fori(0, TILES // 2) as i:
                for par in range(2):
                    turn_tile(i * 2 + par + 1, 1 - par)
                    expert(i * 2 + par, par)
            expert(TILES - 1, 0)

            def add_x1(t, j):
                pe.wait_ge(y_done, t + 1)
                nc.tensor.matmul(st[:, j], ident[:, :], x1_all[:, bass.ds(t * D, D)], start=True, stop=False,
                                 skip_group_check=True)

            def add_experts(t, j):
                pe.wait_ge(got_rows[j], (t // GOT) * 32 + 32)
                nc.tensor.matmul(st[:, j], ident[:, :], got[:, j, 0], start=False, stop=False, skip_group_check=True)
                nc.tensor.matmul(st[:, j], ident[:, :], got[:, j, 1], start=False, stop=True, skip_group_check=True
                                 ).then_inc(sum_ready, 1)

            add_x1(0, 0)
            add_x1(1, 1)
            with pe.Fori(0, NT // GOT - 1) as i:
                for j in range(GOT):
                    t = i * GOT + j
                    add_experts(t, j)
                    add_x1(t + 2, (j + 2) % GOT)
            for t in range(NT - GOT, NT):
                add_experts(t, t % GOT)
                if t + 2 < NT:
                    add_x1(t + 2, (t + 2) % GOT)


def kernel(L0_attn_x, L0_attn_Wq, L0_attn_Wk, L0_attn_Wv, L0_attn_Wo, L0_ffn_W_gate, L0_ffn_b_gate, L0_ffn_W_e, L0_ffn_b_e):
    import numpy as np
    import concourse.bacc as bacc
    from concourse.bass_utils import run_bass_kernel_spmd

    x = np.asarray(L0_attn_x).reshape(T, D)
    wq = np.asarray(L0_attn_Wq).reshape(D, 2, 4, G, 2, HALF).transpose(0, 1, 4, 3, 2, 5).reshape(D, D)
    wk = np.asarray(L0_attn_Wk).reshape(D, HKV, 2, HALF).transpose(0, 2, 1, 3).reshape(D, HKV * DH)
    inv = (1.0 / np.float32(10000.0) ** (np.arange(0, DH, 2, dtype=np.float32) / np.float32(DH))).astype(np.float32)
    ang = np.tile((np.arange(S, dtype=np.float32)[:, None] * inv[None, :]).T, (P // HALF, 1))
    cos, sin = np.cos(ang), np.sin(ang)
    ksin = np.where(np.arange(P)[:, None] < 64, sin, -sin)
    data = {
        "xT": x.T, "x": x, "wq": wq, "wk": wk, "wv": L0_attn_Wv, "wo": L0_attn_Wo, "wg": L0_ffn_W_gate,
        "bg": L0_ffn_b_gate, "we": L0_ffn_W_e, "be": L0_ffn_b_e, "cos": cos, "sin": sin, "ksin": ksin,
    }
    nc = bacc.Bacc("TRN2", target_bir_lowering=False, num_devices=1)
    arrays, args = {}, []
    for name, a in data.items():
        a = np.ascontiguousarray(a)
        arrays[name] = a
        args.append(nc.dram_tensor(name, a.shape, mybir.dt.from_np(a.dtype), kind="ExternalInput").ap())
    out = nc.dram_tensor("out", [T, D], F32, kind="ExternalOutput").ap()
    layer(nc, *args, out)
    r = run_bass_kernel_spmd(nc, [arrays], core_ids=[0])
    return np.asarray(r.results[0]["out"]).reshape(B, S, D)
```
